# Optimizing a Trainium2 kernel written in Bass

```python
import numpy as np
import jax
import jax.numpy as jnp

def _softmax(x, axis=-1):
    return jax.nn.softmax(x, axis=axis)

def _gelu(x):
    return jax.nn.gelu(x, approximate=True)

def _silu(x):
    return jax.nn.silu(x)

def _sigmoid(x):
    return jax.nn.sigmoid(x)

def _layernorm(x, axis=-1, eps=1e-05):
    m = jnp.mean(x, axis=axis, keepdims=True)
    v = jnp.var(x, axis=axis, keepdims=True)
    return (x - m) / jnp.sqrt(v + eps)

def _scatter_add(tgt, idx, src, axis=0):
    return tgt.at[idx].add(src)

def _segment_sum(src, seg, n):
    return jax.ops.segment_sum(src, seg, n)
kernel_name = 'mk_prb_d1_jaxref_r8_f12407'

def setup_inputs(seed: int=0):
    np.random.seed(seed)
    _w = jnp.asarray

    def _L0_attn_setup():
        import jax, jax.numpy as jnp
        import numpy as np
        DT_MIN, DT_MAX = (0.001, 0.1)
        BSZ, SEQ, DM, DS = (8, 256, 128, 16)

        def _depthwise_conv(x, conv_w, conv_b):
            xc = jnp.transpose(x, (0, 2, 1))
            y = jax.lax.conv_general_dilated(xc, conv_w, window_strides=(1,), padding=[(1, 1)], feature_group_count=xc.shape[1], dimension_numbers=('NCH', 'OIH', 'NCH'))
            y = y + conv_b[None, :, None]
            return jnp.transpose(y, (0, 2, 1))
        key = jax.random.key(seed)
        ks = jax.random.split(key, 8)
        x = jax.random.normal(ks[0], (BSZ, SEQ, DM), jnp.float32)
        a_log = jax.random.normal(ks[1], (DM, DS), jnp.float32) * -0.5
        b = jax.random.normal(ks[2], (DM, DS), jnp.float32) * 0.02
        c = jax.random.normal(ks[3], (DM, DS), jnp.float32) * 0.02
        dt_w = jax.random.normal(ks[4], (DM, DM), jnp.float32) * (1.0 / np.sqrt(DM))
        dt_b = jnp.zeros((DM,), jnp.float32)
        conv_w = jax.random.normal(ks[5], (DM, 1, 3), jnp.float32) * (1.0 / np.sqrt(3.0))
        conv_b = jnp.zeros((DM,), jnp.float32)
        return {'x': x, 'a_log': a_log, 'b': b, 'c': c, 'dt_w': dt_w, 'dt_b': dt_b, 'conv_w': conv_w, 'conv_b': conv_b}
    _L0_attn_in = _L0_attn_setup()

    def _L0_ffn_setup():
        import jax, jax.numpy as jnp
        import numpy as np
        QK_SCALE = 10.0
        NEG_INF = -1000000000.0

        def layernorm(x, g, b, eps=1e-05):
            mu = jnp.mean(x, axis=-1, keepdims=True)
            var = jnp.var(x, axis=-1, keepdims=True)
            return (x - mu) * jax.lax.rsqrt(var + eps) * g + b

        def l2norm(x, eps=1e-12):
            return x / jnp.sqrt(jnp.sum(x * x, axis=-1, keepdims=True) + eps)
        key = jax.random.key(seed)
        ks = jax.random.split(key, 10)
        B, S, D, H, DH, E, FF = (2, 128, 128, 16, 64, 8, 512)
        sd = lambda fan: 1.0 / np.sqrt(fan)
        return {'x': jax.random.normal(ks[0], (B, S, D), jnp.float32), 'ln_g': jnp.ones((D,), jnp.float32), 'ln_b': jnp.zeros((D,), jnp.float32), 'Wq': jax.random.normal(ks[1], (D, H * DH), jnp.float32) * sd(D), 'Wk': jax.random.normal(ks[2], (D, H * DH), jnp.float32) * sd(D), 'Wv': jax.random.normal(ks[3], (D, H * DH), jnp.float32) * sd(D), 'q_scale': jnp.ones((H, 1, DH), jnp.float32), 'k_scale': jnp.ones((H, 1, DH), jnp.float32), 'Wo': jax.random.normal(ks[4], (H * DH, D), jnp.float32) * sd(H * DH), 'gate_w': jax.random.normal(ks[5], (D, E), jnp.float32) * sd(D), 'gate_b': jnp.zeros((E,), jnp.float32), 'w1': jax.random.normal(ks[6], (E, D, FF), jnp.float32) * sd(D), 'b1': jnp.zeros((E, FF), jnp.float32), 'w2': jax.random.normal(ks[7], (E, FF, D), jnp.float32) * sd(FF), 'b2': jnp.zeros((E, D), jnp.float32)}
    _L0_ffn_in = _L0_ffn_setup()
    _d = {'L0_attn_x': _L0_attn_in['x'], 'L0_attn_a_log': _L0_attn_in['a_log'], 'L0_attn_b': _L0_attn_in['b'], 'L0_attn_c': _L0_attn_in['c'], 'L0_attn_dt_w': _L0_attn_in['dt_w'], 'L0_attn_dt_b': _L0_attn_in['dt_b'], 'L0_attn_conv_w': _L0_attn_in['conv_w'], 'L0_attn_conv_b': _L0_attn_in['conv_b'], 'L0_ffn_ln_g': _L0_ffn_in['ln_g'], 'L0_ffn_ln_b': _L0_ffn_in['ln_b'], 'L0_ffn_Wq': _L0_ffn_in['Wq'], 'L0_ffn_Wk': _L0_ffn_in['Wk'], 'L0_ffn_Wv': _L0_ffn_in['Wv'], 'L0_ffn_q_scale': _L0_ffn_in['q_scale'], 'L0_ffn_k_scale': _L0_ffn_in['k_scale'], 'L0_ffn_Wo': _L0_ffn_in['Wo'], 'L0_ffn_gate_w': _L0_ffn_in['gate_w'], 'L0_ffn_gate_b': _L0_ffn_in['gate_b'], 'L0_ffn_w1': _L0_ffn_in['w1'], 'L0_ffn_b1': _L0_ffn_in['b1'], 'L0_ffn_w2': _L0_ffn_in['w2'], 'L0_ffn_b2': _L0_ffn_in['b2']}
    _x0 = _d['L0_attn_x']
    _d['L0_attn_x'] = jax.random.normal(jax.random.fold_in(jax.random.key(seed), 1), (16, 256, 128), dtype=_x0.dtype)
    del _x0
    return _d

def reference(L0_attn_x, L0_attn_a_log, L0_attn_b, L0_attn_c, L0_attn_dt_w, L0_attn_dt_b, L0_attn_conv_w, L0_attn_conv_b, L0_ffn_ln_g, L0_ffn_ln_b, L0_ffn_Wq, L0_ffn_Wk, L0_ffn_Wv, L0_ffn_q_scale, L0_ffn_k_scale, L0_ffn_Wo, L0_ffn_gate_w, L0_ffn_gate_b, L0_ffn_w1, L0_ffn_b1, L0_ffn_w2, L0_ffn_b2):

    def _L0_attn_ref(x, a_log, b, c, dt_w, dt_b, conv_w, conv_b):
        import jax, jax.numpy as jnp
        import numpy as np
        DT_MIN, DT_MAX = (0.001, 0.1)
        BSZ, SEQ, DM, DS = (8, 256, 128, 16)

        def _depthwise_conv(x, conv_w, conv_b):
            xc = jnp.transpose(x, (0, 2, 1))
            y = jax.lax.conv_general_dilated(xc, conv_w, window_strides=(1,), padding=[(1, 1)], feature_group_count=xc.shape[1], dimension_numbers=('NCH', 'OIH', 'NCH'))
            y = y + conv_b[None, :, None]
            return jnp.transpose(y, (0, 2, 1))
        Bn, N, C = x.shape
        D = a_log.shape[1]
        xf = _depthwise_conv(x, conv_w, conv_b)
        dt = jax.nn.sigmoid(xf @ dt_w.T + dt_b) * (DT_MAX - DT_MIN) + DT_MIN
        A = -jax.nn.softplus(a_log)

        def step(s, inp):
            xt, dtt = inp
            expA = jnp.exp(dtt[..., None] * A)
            s = expA * s + (dtt * xt)[..., None] * b
            y = jnp.einsum('bcd,cd->bc', s, c)
            return (s, y)
        s0 = jnp.zeros((Bn, C, D), x.dtype)
        xs = (jnp.transpose(xf, (1, 0, 2)), jnp.transpose(dt, (1, 0, 2)))
        _, ys = jax.lax.scan(step, s0, xs)
        return jnp.transpose(ys, (1, 0, 2))

    def _L0_ffn_ref(x, ln_g, ln_b, Wq, Wk, Wv, q_scale, k_scale, Wo, gate_w, gate_b, w1, b1, w2, b2):
        import jax, jax.numpy as jnp
        import numpy as np
        QK_SCALE = 10.0
        NEG_INF = -1000000000.0

        def layernorm(x, g, b, eps=1e-05):
            mu = jnp.mean(x, axis=-1, keepdims=True)
            var = jnp.var(x, axis=-1, keepdims=True)
            return (x - mu) * jax.lax.rsqrt(var + eps) * g + b

        def l2norm(x, eps=1e-12):
            return x / jnp.sqrt(jnp.sum(x * x, axis=-1, keepdims=True) + eps)
        B, S, D = x.shape
        H = q_scale.shape[0]
        DH = q_scale.shape[-1]
        h = layernorm(x, ln_g, ln_b)
        q = (h @ Wq).reshape(B, S, H, DH).transpose(0, 2, 1, 3)
        k = (h @ Wk).reshape(B, S, H, DH).transpose(0, 2, 1, 3)
        v = (h @ Wv).reshape(B, S, H, DH).transpose(0, 2, 1, 3)
        q = l2norm(q) * q_scale
        k = l2norm(k) * k_scale
        logits = jnp.einsum('bhid,bhjd->bhij', q, k) * QK_SCALE
        causal = jnp.tril(jnp.ones((S, S), bool))
        logits = jnp.where(causal, logits, NEG_INF)
        attn = jax.nn.softmax(logits, axis=-1)
        out = jnp.einsum('bhij,bhjd->bhid', attn, v)
        out = out.transpose(0, 2, 1, 3).reshape(B, S, H * DH) @ Wo
        h = layernorm(out, ln_g, ln_b)
        gate = jax.nn.softmax(h @ gate_w + gate_b, axis=-1)
        hid = jax.nn.gelu(jnp.einsum('bsd,edf->bsef', h, w1) + b1)
        exp_out = jnp.einsum('bsef,efd->bsed', hid, w2) + b2
        moe = jnp.einsum('bse,bsed->bsd', gate, exp_out)
        return layernorm(moe, ln_g, ln_b)
    x = L0_attn_x
    xn = _layernorm(x, axis=-1)
    x = x + _L0_attn_ref(xn, L0_attn_a_log, L0_attn_b, L0_attn_c, L0_attn_dt_w, L0_attn_dt_b, L0_attn_conv_w, L0_attn_conv_b) + _L0_ffn_ref(xn, L0_ffn_ln_g, L0_ffn_ln_b, L0_ffn_Wq, L0_ffn_Wk, L0_ffn_Wv, L0_ffn_q_scale, L0_ffn_k_scale, L0_ffn_Wo, L0_ffn_gate_w, L0_ffn_gate_b, L0_ffn_w1, L0_ffn_b1, L0_ffn_w2, L0_ffn_b2)
    return x

_drawn_inputs = setup_inputs


def setup_inputs(seed=0):
    import zlib

    import numpy as np

    out = dict(_drawn_inputs(seed))
    spreads = {'L0_attn_dt_b': (0.0, 0.8),
     'L0_attn_conv_b': (0.0, 0.8),
     'L0_ffn_ln_g': (1.0, 0.2),
     'L0_ffn_ln_b': (0.0, 0.1),
     'L0_ffn_q_scale': (1.0, 0.2),
     'L0_ffn_k_scale': (1.0, 0.2),
     'L0_ffn_gate_b': (0.0, 0.1),
     'L0_ffn_b1': (0.0, 0.1),
     'L0_ffn_b2': (0.0, 0.1)}
    factors = {'L0_attn_a_log': 8.0,
     'L0_attn_b': 8.0,
     'L0_attn_c': 8.0,
     'L0_attn_dt_w': 8.0,
     'L0_attn_conv_w': 8.0}
    for name, (base, spread) in spreads.items():
        noise = np.random.default_rng([zlib.crc32(name.encode()), seed]).standard_normal(out[name].shape)
        drawn = base * np.exp(spread * noise) if base else spread * noise
        out[name] = jnp.asarray(drawn.astype(out[name].dtype))
    for name, factor in factors.items():
        out[name] = (out[name] * factor).astype(out[name].dtype)
    return out
```

```python
from contextlib import ExitStack

import numpy as np
import concourse.bass as bass
from concourse import mybir
from concourse.alu_op_type import AluOpType as ALU

F32 = mybir.dt.float32
F16 = mybir.dt.float16
BF16 = mybir.dt.bfloat16
ACT = mybir.ActivationFunctionType
AX = mybir.AxisListType

NSEQ, SEQ, D = 16, 256, 128
P = 128
T = SEQ // P
H, DH = 16, 64
HD = H * DH
NE, FF = 8, 512
FC = FF // P
DS = 16
GH = 4
NG = H // GH
PC = SEQ + P
NJ = 4 * T
NT = 5 * T
WS = 64.0
LN_EPS, L2_EPS = 1e-5, 1e-12
QK_SCALE = 10.0
DT_MIN, DT_MAX = 0.001, 0.1
MASKED = -1e9
LAST = NSEQ - 1

KG, KGA = 24, 4
KN = 5
KO, KOA = 22, 4
KE = 12
KC = 5


def build(nc, x, a_log, b, c, dt_w, dt_b, conv_w, conv_b, ln_g, ln_b, Wq, Wk, Wv, q_scale, k_scale,
          Wo, gate_w, gate_b, w1, b1, w2, b2, out):
    ctx = ExitStack()
    with ctx:
        def sb(name, shape, dt=F32):
            return ctx.enter_context(nc.sbuf_tensor(name, shape, dt))

        def sem(name):
            return ctx.enter_context(nc.semaphore(name))

        ident = sb("ident", [P, P])
        ident16 = sb("ident16", [P, P], F16)
        identb = sb("identb", [P, P], BF16)
        mask = sb("mask", [P, P])
        maskb = sb("maskb", [P, P], BF16)
        wh = sb("wh", [P, 3 * HD], F16)
        wl = sb("wl", [P, 3 * HD], F16)
        w1h = sb("w1h", [P, NE * FF], F16)
        w1l = sb("w1l", [P, NE * FF], F16)
        w2s = sb("w2s", [P, NE * FC, D])
        wos = sb("wos", [P, HD // P, D])
        crow = sb("crow", [P, HD])
        dtw = sb("dtw", [P, D])
        dtwT = sb("dtwT", [P, D])
        b1r = sb("b1r", [NE * FC, P])
        b1c = sb("b1c", [P, NE * FC])
        cols = sb("cols", [P, 8])
        lng, lnb, dtb, cb = (cols[:, n:n + 1] for n in range(4))
        half_dtb = sb("half_dtb", [P, 1])
        grow = sb("grow", [P, D])
        brow = sb("brow", [P, D])
        gbrow = sb("gbrow", [P, NE])
        gws = sb("gws", [P, NE])
        b2s = sb("b2s", [NE, D])
        al = sb("al", [P, DS])
        bs = sb("bs", [P, DS])
        cs = sb("cs", [P, DS])
        bc = sb("bc", [P, DS])
        spt = sb("spt", [P, 4, DS])
        negA = sb("negA", [P, DS])
        eps_ln = sb("eps_ln", [P, 1])
        eps_l2 = sb("eps_l2", [P, 1])
        pad = sb("pad", [P, 1])
        xin = sb("xin", [P, T, D])
        xn = sb("xn", [P, T, D])
        z = sb("z", [P, T, D])
        gst = sb("gst", [P, T, 6])
        gmv = sb("gmv", [P, T, 2])
        gve = sb("gve", [P, T])
        gln = sb("gln", [P, T])
        gy = sb("gy", [P, T])
        gu = sb("gu", [P, T])
        gw = sb("gw", [P, T])
        gr = sb("gr", [P, T])
        xnT = sb("xnT", [P, SEQ + 2])
        hT = sb("hT", [P, SEQ])
        hTh = sb("hTh", [P, SEQ], F16)
        hTl = sb("hTl", [P, SEQ], F16)
        raw = sb("raw", [P, NJ, 512])
        sq = sb("sq", [P, 2, 512])
        ssq = sb("ssq", [P, NJ * 8])
        nve = sb("nve", [P, NJ * 8])
        nln = sb("nln", [P, NJ * 8])
        ny = sb("ny", [P, NJ * 8])
        nu = sb("nu", [P, NJ * 8])
        nw = sb("nw", [P, NJ * 8])
        nr = sb("nr", [P, NJ * 8])
        rq10 = sb("rq10", [P, T, H])
        qc = sb("qc", [P, 2, 512])
        Qs = sb("Qs", [P, T, H // 2, 4, DH], F16)
        Kh = sb("Kh", [P, T, H, 2, DH], F16)
        Kl = sb("Kl", [P, T, HD], F16)
        QT = sb("QT", [P, H, SEQ], F16)
        KT = sb("KT", [P, H, SEQ], F16)
        KL = sb("KL", [P, H // 2, SEQ], F16)
        Vh = sb("Vh", [P, T, HD], F16)
        Vl = sb("Vl", [P, T, HD], F16)
        mx = sb("mx", [P, 2, T])
        nb = sb("nb", [P, 2, T])
        P32 = sb("P32", [P, 3, PC])
        Ph = sb("Ph", [P, 2, PC], F16)
        Pl = sb("Pl", [P, 2, PC], F16)
        PT = sb("PT", [P, 2, 2, 3, P], F16)
        rs = sb("rs", [P, NG, T, GH])
        rr = sb("rr", [P, 2, T * GH])
        On = sb("On", [P, 2, T, GH * DH])
        OT = sb("OT", [P, HD // P, SEQ])
        ost = sb("ost", [P, T, 6])
        omv = sb("omv", [P, T, 2])
        ove = sb("ove", [P, T])
        oln = sb("oln", [P, T])
        oy = sb("oy", [P, T])
        ou = sb("ou", [P, T])
        ow = sb("ow", [P, T])
        orr = sb("orr", [P, T])
        z2 = sb("z2", [P, T, D])
        h2T = sb("h2T", [P, SEQ])
        h2h = sb("h2h", [P, SEQ], F16)
        h2l = sb("h2l", [P, SEQ], F16)
        gl = sb("gl", [P, T, NE])
        gm = sb("gm", [P, T])
        ge = sb("ge", [P, T, NE])
        gs = sb("gs", [P, T])
        grs = sb("grs", [P, T])
        gate = sb("gate", [P, T, P])
        gateT = sb("gateT", [P, SEQ])
        hid = sb("hid", [P, 2, FC, SEQ])
        acc = sb("acc", [P, T, D])
        aexp = sb("aexp", [P, DS, SEQ])
        xf = sb("xf", [P, SEQ])
        cv = sb("cv", [P, 2, SEQ])
        th = sb("th", [P, SEQ])
        dt = sb("dt", [P, SEQ])
        u = sb("u", [P, SEQ])
        st = sb("st", [P, 2, SEQ])
        y = sb("y", [P, SEQ])
        est = sb("est", [P, T, 6])
        emv = sb("emv", [P, T, 2])
        eve = sb("eve", [P, T])
        eln = sb("eln", [P, T])
        ey = sb("ey", [P, T])
        eu = sb("eu", [P, T])
        ew = sb("ew", [P, T])
        er = sb("er", [P, T])
        e1 = sb("e1", [P, T, D])
        e2 = sb("e2", [P, T, D])
        xy = sb("xy", [P, T, D])
        fin = sb("fin", [P, T, D])
        xres = sb("xres", [P, T, D])
        xb = sb("xb", [P, T, D])
        krow = sq[:, :, :].rearrange("p a n -> p (a n)")
        W32 = raw[:, 0:6, :].rearrange("p a n -> p (a n)")
        W132 = aexp[:, :, :].rearrange("p a n -> p (a n)")

        bank = [ctx.enter_context(nc.psum_tensor(f"bank{n}", [P, 512], F32)) for n in range(8)]
        score_b = bank[0:2]
        turn_b = bank[2:4]
        sum_b = bank[4:6]
        misc_b = bank[6:8]

        names = """d_small d_w d_w1 d_w2 d_wo d_rows x_loaded xres_loaded fin_free
            const_pool const_vec w_high w_low w1_high w1_low setup_tr setup_vec setup_act
            g_vec g_act g_tr
            qk_ready qk_raw qk_sq qk_sum qc_done q_hi q_lo n_vec n_act k_norm k_hi k_lo
            v_ready v_hi v_lo t_ready t_even t_odd
            sc_ready mx_done nb_done ex_done p_hi p_lo pt_ready pt_even pt_odd pv_done rr_done on_done
            ot_ready ot_done
            wo_ready o_vec o_act o_tr o_gate o_gT o_b2
            w1_ready gelu_done w2_ready acc_done
            c_vec dt_ready tanh_done a_done scan_done y_done
            y_tr e_vec e_act xb_done xy_done""".split()
        S = {n: sem(n) for n in names}
        (d_small, d_w, d_w1, d_w2, d_wo, d_rows, x_loaded, xres_loaded, fin_free,
         const_pool, const_vec, w_high, w_low, w1_high, w1_low, setup_tr, setup_vec, setup_act,
         g_vec, g_act, g_tr,
         qk_ready, qk_raw, qk_sq, qk_sum, qc_done, q_hi, q_lo, n_vec, n_act, k_norm, k_hi, k_lo,
         v_ready, v_hi, v_lo, t_ready, t_even, t_odd,
         sc_ready, mx_done, nb_done, ex_done, p_hi, p_lo, pt_ready, pt_even, pt_odd, pv_done, rr_done, on_done,
         ot_ready, ot_done,
         wo_ready, o_vec, o_act, o_tr, o_gate, o_gT, o_b2,
         w1_ready, gelu_done, w2_ready, acc_done,
         c_vec, dt_ready, tanh_done, a_done, scan_done, y_done,
         y_tr, e_vec, e_act, xb_done, xy_done) = (S[n] for n in names)

        def tiles(ap):
            return ap.rearrange("(t p) d -> p t d", p=P)

        def turned(n):
            src = turn_b[n % 2][:, :].bitcast(F16).rearrange("p (m q) -> p m q", q=P)
            if n < 8:
                t, h = (n % 4) // 2, (n % 2) * 8
                return (QT, KT)[n // 4][:, h:h + 8, t * P:(t + 1) * P], src
            return KL[:, :, (n - 8) * P:(n - 7) * P], src

        def bodies(eng, prologue, body, tail):
            prologue()
            body(0, older=False, old=False, new=True, newer=True)
            body(1, older=False, old=True, new=True, newer=True)
            with eng.Fori(2, NSEQ - 2) as i:
                body(i, older=True, old=True, new=True, newer=True)
            body(NSEQ - 2, older=True, old=True, new=True, newer=False)
            body(LAST, older=True, old=True, new=False, newer=False)
            tail()

        def from_one(eng, semaphore, value):
            if not isinstance(value, int) or value > 0:
                eng.wait_ge(semaphore, value)

        block = ctx.enter_context(nc.Block())

        @block.sync
        def _(sp):
            def load_x(s):
                if not isinstance(s, int) or s > 0:
                    sp.wait_ge(g_vec, (s - 1) * KG + 10)
                sp.dma_start(xin[:, :, :], tiles(x[s])).then_inc(x_loaded, 16)

            def load_xres(s):
                if not isinstance(s, int) or s > 0:
                    sp.wait_ge(xb_done, s)
                sp.dma_start(xres[:, :, :], tiles(x[s])).then_inc(xres_loaded, 16)

            def store_out(s):
                sp.wait_ge(e_vec, (s + 1) * KE)
                sp.dma_start(tiles(out[s]), fin[:, :, :]).then_inc(fin_free, 16)

            def prologue():
                load_x(0)
                load_xres(0)
                for n, w in enumerate((Wq, Wk, Wv)):
                    sp.dma_start(W32[:, n * HD:(n + 1) * HD], w).then_inc(d_w, 16)
                load_x(1)
                sp.dma_start(W132.rearrange("p (e f) -> p e f", e=NE),
                             w1.rearrange("e p f -> p e f")).then_inc(d_w1, 16)
                sp.dma_start(w2s[:, :, :].rearrange("p (e c) n -> p e c n", e=NE),
                             w2.rearrange("e (c p) n -> p e c n", p=P)).then_inc(d_w2, 16)

            def body(i, older, old, new, newer):
                if newer:
                    load_x(i + 2)
                if old:
                    load_xres(i)
                if older:
                    store_out(i - 2)

            def tail():
                store_out(LAST - 1)
                store_out(LAST)
                sp.wait_ge(fin_free, 16 * (NSEQ + 1))

            bodies(sp, prologue, body, tail)

        @block.tensor
        def _(pe):
            mm, tr = nc.tensor.matmul, nc.tensor.transpose

            def turn(s):
                pe.wait_ge(g_vec, s * KG + 20)
                for t in range(T):
                    tr(misc_b[0][:, t * P:(t + 1) * P], xn[:, t, :], ident[:, :])
                for t in range(T):
                    last = tr(misc_b[0][:, SEQ + t * P:SEQ + (t + 1) * P], z[:, t, :], ident[:, :])
                last.then_inc(g_tr, 1)

            def split(dst, s, t, w0, ready):
                hi, lo = hTh[:, t * P:(t + 1) * P], hTl[:, t * P:(t + 1) * P]
                mm(dst, hi, wh[:, w0:w0 + 512], start=True, stop=False)
                mm(dst, lo, wh[:, w0:w0 + 512], start=False, stop=False)
                mm(dst, hi, wl[:, w0:w0 + 512], start=False, stop=True).then_inc(ready, 1)

            def project(s, j):
                if j == 0:
                    pe.wait_ge(g_vec, (s + 1) * KG)
                if j >= 2:
                    pe.wait_ge(qk_raw, s * NJ + j - 1)
                t, w = divmod(j, 4)
                split(misc_b[j % 2][:, :], s, t, w * 512, qk_ready)

            def project_v(s, j):
                if j == 0:
                    pe.wait_ge(qk_raw, (s + 1) * NJ)
                    from_one(pe, o_vec, (s - 1) * KO)
                if j >= 2:
                    pe.wait_ge(v_lo, s * 2 * T + j - 1)
                t, w = divmod(j, 2)
                split(misc_b[j % 2][:, :], s, t, 2 * HD + w * 512, v_ready)

            def turn_qk(s, n):
                if n == 0:
                    pe.wait_ge(q_lo, (s + 1) * 2 * T)
                if n == 4:
                    pe.wait_ge(k_lo, (s + 1) * 2 * T)
                if n >= 2:
                    pe.wait_ge((t_even, t_odd)[n % 2], s * (NT // 2) + n // 2)
                dst = turn_b[n % 2][:, :].bitcast(F16)
                for m in range(8):
                    if n < 8:
                        t, h = (n % 4) // 2, (n % 2) * 8 + m
                    if n < 4:
                        src = Qs[:, t, h // 2, 2 * (h % 2):2 * (h % 2) + 2, :].rearrange("p a d -> p (a d)")
                    elif n < 8:
                        src = Kh[:, t, h, :, :].rearrange("p a d -> p (a d)")
                    else:
                        src = Kl[:, n - 8, m * P:(m + 1) * P]
                    last = tr(dst[:, m * P:(m + 1) * P], src, ident16[:, :])
                last.then_inc(t_ready, 1)

            def scores(s, h, before):
                if h == 0:
                    pe.wait_ge(t_even, (s + 1) * (NT // 2))
                    pe.wait_ge(t_odd, (s + 1) * (NT // 2))
                    if before:
                        pe.wait_ge(gelu_done, (s - 1) * NE * FC)
                if h >= 2:
                    pe.wait_ge(ex_done, s * 2 * H + 2 * (h - 1))
                o, p0 = score_b[h % 2], DH * (h % 2)
                for t in range(T):
                    keys = (t + 1) * P
                    dst = o[:, t * P:t * P + keys]
                    q = QT[:, h, t * P:(t + 1) * P]
                    mm(dst, q, KT[:, h, 0:keys], start=True, stop=False)
                    mm(dst, q[p0:p0 + DH, :], KL[p0:p0 + DH, h // 2, 0:keys], start=False, stop=False)
                    last = mm(dst[:, t * P:keys], identb[:, :], maskb[:, :], start=False, stop=True)
                last.then_inc(sc_ready, 1)

            def turn_p(s, h):
                pe.wait_ge(p_lo, s * H + h + 1)
                dst = turn_b[h % 2][:, :].bitcast(F16)
                for n, src in enumerate((Ph, Pl)):
                    for m in range(3):
                        last = tr(dst[:, (3 * n + m) * P:(3 * n + m + 1) * P],
                                  src[:, h % 2, m * P:(m + 1) * P], ident16[:, :])
                last.then_inc(pt_ready, 1)

            def weigh(s, h, before):
                g = h // GH
                pe.wait_ge((pt_even, pt_odd)[h % 2], s * (H // 2) + h // 2 + 1)
                if h == 0:
                    pe.wait_ge(v_lo, (s + 1) * 2 * T)
                    if before:
                        pe.wait_ge(acc_done, (s - 1) * NE * T)
                if h % GH == 0 and g >= 2:
                    pe.wait_ge(ot_done, s * NG + g - 1)
                for t in range(T):
                    dst = sum_b[g % 2][:, (t * GH + h % GH) * DH:(t * GH + h % GH + 1) * DH]
                    terms = [(a, kb) for kb in range(t + 1) for a in ((0, Vh), (0, Vl), (1, Vh))]
                    for n, ((half, v), kb) in enumerate(terms):
                        last = mm(dst, PT[:, h % 2, half, t + kb, :], v[:, kb, h * DH:(h + 1) * DH],
                                  start=(n == 0), stop=(n == len(terms) - 1))
                last.then_inc(pv_done, 1)

            def turn_o(s, g):
                pe.wait_ge(on_done, s * NG + g + 1)
                for m in range(2):
                    for t in range(T):
                        last = tr(sum_b[g % 2][:, (m * T + t) * P:(m * T + t + 1) * P],
                                  On[:, g % 2, t, m * P:(m + 1) * P], ident[:, :])
                last.then_inc(ot_ready, 1)

            def output(s, part):
                o0, o1 = misc_b
                if part < T:
                    t = part
                    if t == 0:
                        pe.wait_ge(ot_done, (s + 1) * NG)
                    for m in range(HD // P):
                        last = mm(o0[:, t * P:(t + 1) * P], OT[:, m, t * P:(t + 1) * P],
                                  wos[:, m, :], start=(m == 0), stop=(m == HD // P - 1))
                    if t == T - 1:
                        last.then_inc(wo_ready, 1)
                elif part == 2:
                    pe.wait_ge(o_vec, s * KO + 10)
                    for t in range(T):
                        last = tr(o1[:, t * P:(t + 1) * P], z2[:, t, :], ident[:, :])
                    last.then_inc(o_tr, 1)
                elif part == 3:
                    pe.wait_ge(o_vec, s * KO + 11)
                    for t in range(T):
                        last = mm(o0[:, t * NE:(t + 1) * NE], h2T[:, t * P:(t + 1) * P], gws[:, :],
                                  start=True, stop=True)
                    last.then_inc(o_gate, 1)
                elif part == 4:
                    pe.wait_ge(o_vec, s * KO + 20)
                    for t in range(T):
                        last = tr(o1[:, t * P:(t + 1) * P], gate[:, t, :], ident[:, :])
                    last.then_inc(o_gT, 1)
                else:
                    pe.wait_ge(o_vec, s * KO + 21)
                    for t in range(T):
                        last = mm(o0[:, t * P:(t + 1) * P], gateT[0:NE, t * P:(t + 1) * P], b2s[:, :],
                                  start=True, stop=True)
                    last.then_inc(o_b2, 1)

            def expert_up(s, e):
                if e == 0:
                    pe.wait_ge(o_vec, s * KO + 13)
                for q in (2 * e, 2 * e + 1):
                    if q >= 2:
                        pe.wait_ge(gelu_done, s * NE * FC + 2 * (q - 1))
                    for m in range(2):
                        f = (2 * q + m) * P
                        dst = score_b[q % 2][:, m * SEQ:(m + 1) * SEQ]
                        mm(dst, w1h[:, f:f + P], h2h[:, :], start=True, stop=False)
                        mm(dst, w1h[:, f:f + P], h2l[:, :], start=False, stop=False)
                        last = mm(dst, w1l[:, f:f + P], h2h[:, :], start=False, stop=True)
                    last.then_inc(w1_ready, 1)

            def expert_down(s, e):
                pe.wait_ge(gelu_done, s * NE * FC + FC * (e + 1))
                if e >= 2:
                    pe.wait_ge(acc_done, s * NE * T + T * (e - 1))
                for t in range(T):
                    for m in range(FC):
                        last = mm(sum_b[e % 2][:, t * P:(t + 1) * P], hid[:, e % 2, m, t * P:(t + 1) * P],
                                  w2s[:, e * FC + m, :], start=(m == 0), stop=(m == FC - 1))
                    last.then_inc(w2_ready, 1)

            def step_sizes(s):
                pe.wait_ge(c_vec, s * KC + 3)
                pe.wait_ge(v_lo, (s + 1) * 2 * T)
                mm(misc_b[1][:, 0:SEQ], dtwT[:, :], xf[:, :], start=True, stop=True).then_inc(dt_ready, 1)

            def turn_y(s):
                pe.wait_ge(y_done, (s + 1) * DS)
                for t in range(T):
                    last = tr(misc_b[1][:, t * P:(t + 1) * P], y[:, t * P:(t + 1) * P], ident[:, :])
                last.then_inc(y_tr, 1)

            def heads(i, k, old, older):
                if k < H:
                    scores(i, k, older)
                if 5 <= k < H + 5:
                    weigh(i, k - 5, older)
                if 3 <= k < H + 3:
                    turn_p(i, k - 3)
                if k >= 10 and k % GH == 2 and k < 10 + 4 * NG:
                    turn_o(i, (k - 10) // GH)

            def prologue():
                pe.wait_ge(const_vec, 3)
                pe.wait_ge(d_small, 16 * 17)
                tr(misc_b[1][:, 0:D], dtw[:, :], ident[:, :])
                tr(misc_b[1][:, D:D + NE * FC], b1r[:, :], ident[0:NE * FC, 0:NE * FC]).then_inc(setup_tr, 1)
                turn(0)
                pe.wait_ge(w_low, 1)
                pe.wait_ge(setup_vec, 1)
                for j in range(NJ):
                    project(0, j)
                for j in range(2 * T):
                    project_v(0, j)
                for n in range(NT):
                    turn_qk(0, n)
                pe.wait_ge(v_lo, 2 * T)
                turn(1)
                step_sizes(0)
                pe.wait_ge(w1_low, 1)
                pe.wait_ge(d_w2, 16)
                pe.wait_ge(d_wo, 16)

            def body(i, older, old, new, newer):
                for k in range(H + 1):
                    heads(i, k, old, older)
                    if old and k == 0:
                        pe.wait_ge(tanh_done, i + 1)
                        turn_y(i - 1)
                    if new and 1 <= k < 1 + NJ:
                        if k == 2:
                            if old:
                                pe.wait_ge(xy_done, i)
                            else:
                                pe.wait_ge(tanh_done, i + 1)
                        project(i + 1, k - 1)
                    if old and k == 8:
                        if new:
                            pe.wait_ge(qk_raw, (i + 2) * NJ - 1)
                        output(i - 1, 0)
                    if old and k == 9:
                        output(i - 1, 1)
                    if old and k == 13:
                        if new:
                            pe.wait_ge(qk_raw, (i + 2) * NJ)
                        else:
                            pe.wait_ge(xy_done, i)
                        output(i - 1, 2)
                    if old and k == 15:
                        output(i - 1, 3)
                if old:
                    pe.wait_ge(ex_done, (i + 1) * 2 * H)
                for m in range(NE + 2):
                    for k in (H + 1 + 2 * m, H + 2 + 2 * m):
                        heads(i, k, old, older)
                        if old and k % 2 == 1 and m < NE:
                            expert_up(i - 1, m)
                    if old and m in (0, 1):
                        output(i - 1, 4 + m)
                    if old and 1 <= m <= NE:
                        if m <= 2:
                            pe.wait_ge(ot_done, i * NG + 2 + m)
                        expert_down(i - 1, m - 1)
                    if new and m in (2, 4):
                        project_v(i + 1, m - 2)
                        project_v(i + 1, m - 1)
                    if new and 2 <= m < 7:
                        turn_qk(i + 1, 2 * m - 4)
                        turn_qk(i + 1, 2 * m - 3)
                    if new and m == 6:
                        if newer:
                            pe.wait_ge(v_lo, (i + 2) * 2 * T)
                            turn(i + 2)
                        step_sizes(i + 1)

            def tail():
                pe.wait_ge(o_vec, LAST * KO)
                turn_y(LAST)
                output(LAST, 0)
                output(LAST, 1)
                pe.wait_ge(xy_done, NSEQ)
                for part in range(2, 4):
                    output(LAST, part)
                for e in range(NE + 1):
                    if e < NE:
                        expert_up(LAST, e)
                    if e < 2:
                        output(LAST, 4 + e)
                    if e >= 1:
                        expert_down(LAST, e - 1)

            bodies(pe, prologue, body, tail)

        @block.scalar
        def _(act):
            fn = nc.scalar.activation

            def with_exp_and_ln():
                nc.scalar.preload_act_table_set("natural_log_exp_and_others")

            def with_gelu_and_tanh():
                nc.scalar.preload_act_table_set("gelu_apprx_tanh_and_others")

            def inverse_root(semaphore, at, src, ln, dst, eps):
                fn(ln, src, ACT.Ln, bias=eps).then_inc(semaphore, 1)
                act.wait_ge(semaphore, at + 1)
                fn(dst, ln, ACT.Exp, scale=-0.5).then_inc(semaphore, 1)

            def norm(s, n):
                act.wait_ge(g_vec, s * KG + (4, 14)[n])
                inverse_root(g_act, s * KGA + 2 * n, gmv[:, :, 1], gln[:, :], gy[:, :], eps_ln[:, :])

            def copy_raw(s, j):
                act.wait_ge(qk_ready, s * NJ + j + 1)
                fn(raw[:, j, :], misc_b[j % 2][:, :], ACT.Copy).then_inc(qk_raw, 1)

            def norm_qk(s):
                act.wait_ge(qk_sum, (s + 1) * NJ)
                inverse_root(n_act, s * 2, ssq[:, :], nln[:, :], ny[:, :], eps_l2[:, :])

            def v_high(s, j):
                t, w = divmod(j, 2)
                act.wait_ge(v_ready, s * 2 * T + j + 1)
                fn(Vh[:, t, w * 512:(w + 1) * 512], misc_b[j % 2][:, :], ACT.Copy,
                   scale=1.0 / WS).then_inc(v_hi, 1)

            def copy_turned(s, n):
                act.wait_ge(t_ready, s * NT + n + 1)
                dst, src = turned(n)
                fn(dst, src, ACT.Copy).then_inc(t_odd, 1)

            def root_o(s):
                act.wait_ge(o_vec, s * KO + 4)
                inverse_root(o_act, s * KOA, omv[:, :, 1], oln[:, :], oy[:, :], eps_ln[:, :])

            def gate_exps(s):
                act.wait_ge(o_vec, s * KO + 17)
                for t in range(T):
                    fn(ge[:, t, :], gl[:, t, :], ACT.Exp, accum_out=gs[:, t:t + 1]).then_inc(o_act, 1)

            def exps(s, h):
                act.wait_ge(nb_done, s * H + h + 1)
                if h < 3:
                    from_one(act, p_lo, s * H)
                else:
                    act.wait_ge(p_lo, s * H + h - 2)
                for t in range(T):
                    keys = (t + 1) * P
                    fn(P32[:, h % 3, t * P:t * P + keys], score_b[h % 2][:, t * P:t * P + keys], ACT.Exp,
                       bias=nb[:, h % 2, t:t + 1], scale=rq10[:, t, h:h + 1],
                       accum_out=rs[:, h // GH, t, h % GH:h % GH + 1]).then_inc(ex_done, 1)

            def copy_pt(s, h):
                act.wait_ge(pt_ready, s * H + h + 1)
                from_one(act, pv_done, s * H + h - 1)
                fn(PT[:, h % 2, :, :, :].rearrange("p a b q -> p (a b q)"),
                   turn_b[h % 2][:, :].bitcast(F16)[:, 0:6 * P], ACT.Copy).then_inc(pt_odd, 1)

            def copy_ot(s, g):
                act.wait_ge(ot_ready, s * NG + g + 1)
                if g == 0:
                    from_one(act, wo_ready, s)
                fn(OT[:, 2 * g:2 * g + 2, :].rearrange("p m q -> p (m q)"), sum_b[g % 2][:, :],
                   ACT.Copy).then_inc(ot_done, 1)

            def decay(s, d):
                if d == 0:
                    act.wait_ge(c_vec, s * KC + 5)
                fn(aexp[:, d, :], dt[:, :], ACT.Exp, scale=negA[:, d:d + 1]).then_inc(a_done, 1)

            def step_tanh(s):
                act.wait_ge(dt_ready, s + 1)
                fn(th[:, :], misc_b[1][:, 0:SEQ], ACT.Tanh, bias=half_dtb[:, :], scale=0.5
                   ).then_inc(tanh_done, 1)

            def gelus(s, e):
                for q in (2 * e, 2 * e + 1):
                    act.wait_ge(w1_ready, s * NE * 2 + q + 1)
                    if q % 2 == 0 and e >= 2:
                        act.wait_ge(w2_ready, s * NE * T + T * (e - 1))
                    for m in range(2):
                        f = 2 * q + m
                        fn(hid[:, e % 2, f % FC, :], score_b[q % 2][:, m * SEQ:(m + 1) * SEQ],
                           ACT.Gelu_apprx_tanh, bias=b1c[:, f:f + 1], scale=1.0 / WS).then_inc(gelu_done, 1)

            def last_norm(s):
                act.wait_ge(e_vec, s * KE + 4)
                inverse_root(e_act, s * 2, emv[:, :, 1], eln[:, :], ey[:, :], eps_ln[:, :])

            def prologue():
                for dst, src in ((dtw, dt_w), (b1r, b1.rearrange("e (c p) -> (e c) p", p=P)),
                                 (al, a_log), (bs, b), (cs, c), (gws, gate_w), (b2s, b2)):
                    act.dma_start(dst[:, :], src).then_inc(d_small, 16)
                for n, src in enumerate((ln_g, ln_b, dt_b, conv_b)):
                    act.dma_start(cols[:, n:n + 1], src.unsqueeze(1)).then_inc(d_small, 16)
                act.dma_start(cols[:, 4:7], conv_w.rearrange("p a k -> p (a k)")).then_inc(d_small, 16)
                act.dma_start(grow[:, :], ln_g.partition_broadcast(P)).then_inc(d_small, 16)
                act.dma_start(brow[:, :], ln_b.partition_broadcast(P)).then_inc(d_small, 16)
                act.dma_start(gbrow[:, :], gate_b.partition_broadcast(P)).then_inc(d_small, 16)
                act.dma_start(crow[:, :], q_scale.rearrange("h a d -> (h a d)").partition_broadcast(P)
                              ).then_inc(d_small, 16)
                act.dma_start(krow, k_scale.rearrange("h a d -> (h a d)").partition_broadcast(P)
                              ).then_inc(d_small, 16)
                act.dma_start(wos[:, :, :], Wo.rearrange("(c p) n -> p c n", p=P)).then_inc(d_wo, 16)
                with_exp_and_ln()
                act.wait_ge(const_vec, 3)
                norm(0, 0)
                act.wait_ge(d_w, 48)
                fn(wh[:, :], W32, ACT.Copy, scale=WS).then_inc(w_high, 1)
                norm(0, 1)
                act.wait_ge(d_small, 16 * 17)
                fn(spt[:, 0, :], al[:, :], ACT.Abs).then_inc(setup_act, 1)
                act.wait_ge(setup_act, 1)
                fn(spt[:, 1, :], spt[:, 0, :], ACT.Exp, scale=-1.0).then_inc(setup_act, 1)
                act.wait_ge(setup_act, 2)
                fn(spt[:, 2, :], spt[:, 1, :], ACT.Ln, bias=1.0).then_inc(setup_act, 1)
                act.wait_ge(w_low, 1)
                for j in range(NJ):
                    copy_raw(0, j)
                norm_qk(0)
                act.wait_ge(d_w1, 16)
                fn(w1h[:, :], W132, ACT.Copy, scale=WS).then_inc(w1_high, 1)
                act.wait_ge(setup_vec, 4)
                for j in range(2 * T):
                    v_high(0, j)
                for n in range(1, NT, 2):
                    copy_turned(0, n)
                norm(1, 0)
                norm(1, 1)
                with_gelu_and_tanh()
                step_tanh(0)
                with_exp_and_ln()

            def heads(i, k):
                if 4 <= k < H + 4 and k % 2 == 1:
                    copy_pt(i, k - 4)
                if k in (11, 15, 19):
                    copy_ot(i, (k - 11) // GH)
                if k == 22:
                    copy_ot(i, NG - 1)

            def body(i, older, old, new, newer):
                for k in range(H + 1):
                    if older and k == 1:
                        last_norm(i - 2)
                    if new and 2 <= k < 2 + NJ:
                        copy_raw(i + 1, k - 2)
                    heads(i, k)
                    if new and k == 12:
                        norm_qk(i + 1)
                    if old and k == 11:
                        root_o(i - 1)
                    if newer and k == 10:
                        norm(i + 2, 0)
                    if newer and k == 13:
                        norm(i + 2, 1)
                    if k >= 1:
                        exps(i, k - 1)
                        decay(i, k - 1)
                if old:
                    gate_exps(i - 1)
                with_gelu_and_tanh()
                for m in range(NE + 2):
                    if new and m in (3, 5):
                        v_high(i + 1, m - 3)
                        v_high(i + 1, m - 2)
                    if new and 3 <= m < 8:
                        copy_turned(i + 1, 2 * m - 5)
                    for k in (H + 1 + 2 * m, H + 2 + 2 * m):
                        heads(i, k)
                    if old and m < NE:
                        gelus(i - 1, m)
                    if new and m == 7:
                        step_tanh(i + 1)
                with_exp_and_ln()

            def tail():
                last_norm(LAST - 1)
                root_o(LAST)
                gate_exps(LAST)
                with_gelu_and_tanh()
                for e in range(NE):
                    gelus(LAST, e)
                with_exp_and_ln()
                last_norm(LAST)

            bodies(act, prologue, body, tail)

        @block.gpsimd
        def _(pool):
            def square(s, j):
                pool.wait_ge(qk_raw, s * NJ + j + 1)
                from_one(pool, qk_sum, s * NJ + j - 1)
                nc.gpsimd.tensor_tensor(sq[:, j % 2, :], raw[:, j, :], raw[:, j, :], ALU.mult
                                        ).then_inc(qk_sq, 1)

            def q_low(s, n):
                t, w = divmod(n, 2)
                pool.wait_ge(q_hi, s * 2 * T + n + 1)
                pair = Qs[:, t, 4 * w:4 * w + 4, :, :]
                src = qc[:, n % 2, :].rearrange("p (a h d) -> p a h d", h=2, d=DH)
                nc.gpsimd.tensor_tensor(pair[:, :, 1:3, :], src, pair[:, :, 0:4:3, :], ALU.subtract
                                        ).then_inc(q_lo, 1)

            def k_unit(s, n):
                t, w = divmod(n, 2)
                if n == 0:
                    pool.wait_ge(n_vec, s * KN + 4)
                c0 = t * 2 * H + H + w * 8
                nc.gpsimd.tensor_tensor(
                    raw[:, 4 * t + 2 + w, :].rearrange("p (h d) -> p h d", d=DH),
                    raw[:, 4 * t + 2 + w, :].rearrange("p (h d) -> p h d", d=DH),
                    nr[:, c0:c0 + 8].unsqueeze(2).broadcast_to([P, 8, DH]), ALU.mult).then_inc(k_norm, 1)

            def k_low(s, n):
                t, w = divmod(n, 2)
                pool.wait_ge(k_hi, s * 2 * T + n + 1)
                nc.gpsimd.tensor_tensor(
                    Kl[:, t, w * 512:(w + 1) * 512].rearrange("p (h d) -> p h d", d=DH),
                    raw[:, 4 * t + 2 + w, :].rearrange("p (h d) -> p h d", d=DH),
                    Kh[:, t, w * 8:(w + 1) * 8, 0, :], ALU.subtract).then_inc(k_lo, 1)

            def p_low(s, h):
                pool.wait_ge(p_hi, s * H + h + 1)
                nc.gpsimd.tensor_tensor(Pl[:, h % 2, :], P32[:, h % 3, :], Ph[:, h % 2, :], ALU.subtract
                                        ).then_inc(p_lo, 1)

            def x_bias(s):
                pool.wait_ge(xres_loaded, 16 * (s + 1))
                from_one(pool, xy_done, s)
                nc.gpsimd.tensor_tensor(xb[:, :, :], xres[:, :, :],
                                        brow[:, :].unsqueeze(1).broadcast_to([P, T, D]), ALU.add
                                        ).then_inc(xb_done, 1)

            def prologue():
                nc.gpsimd.memset(ident[:, :], 0.0).then_inc(const_pool, 1)
                nc.gpsimd.memset(mask[:, :], 0.0).then_inc(const_pool, 1)
                pool.wait_ge(const_pool, 2)
                nc.gpsimd.affine_select(out=ident[:, :], in_=ident[:, :], compare_op=ALU.not_equal, fill=1.0,
                                        base=0, pattern=[[-1, P]], channel_multiplier=1
                                        ).then_inc(const_pool, 1)
                nc.gpsimd.affine_select(out=mask[:, :], in_=mask[:, :], compare_op=ALU.is_ge, fill=MASKED,
                                        base=0, pattern=[[-1, P]], channel_multiplier=1
                                        ).then_inc(const_pool, 1)
                pool.wait_ge(d_small, 16 * 17)
                pool.wait_ge(setup_vec, 2)
                for j in range(NJ):
                    square(0, j)
                    if j % 4 == 3:
                        q_low(0, 2 * (j // 4))
                        q_low(0, 2 * (j // 4) + 1)
                for n in range(2 * T):
                    k_unit(0, n)
                for n in range(2 * T):
                    k_low(0, n)

            def body(i, older, old, new, newer):
                for k in range(H + 2):
                    if old and k == 0:
                        x_bias(i - 1)
                    if new and 3 <= k < 3 + NJ:
                        square(i + 1, k - 3)
                    if new and k in (5, 6, 9, 10):
                        q_low(i + 1, (5, 6, 9, 10).index(k))
                    if new and k in (14, 15):
                        k_unit(i + 1, 2 * k - 28)
                        k_unit(i + 1, 2 * k - 27)
                    if 2 <= k:
                        p_low(i, k - 2)
                if new:
                    for n in range(2 * T):
                        k_low(i + 1, n)

            def tail():
                x_bias(LAST)

            bodies(pool, prologue, body, tail)

        @block.vector
        def _(dve):
            V = nc.vector

            def chain(semaphore, s, per):
                n = [0]

                def step(*ins):
                    for one in ins:
                        one.then_inc(semaphore, 1)
                    n[0] += len(ins)
                    assert n[0] <= per
                    dve.wait_ge(semaphore, s * per + n[0])

                def skip(done):
                    n[0] = done
                return step, skip

            def refine(step, root_ready, ve, y0, a, b_, dst, src, eps):
                step(V.tensor_scalar(ve, src, eps, None, ALU.add))
                dve.wait_ge(*root_ready)
                step(V.scalar_tensor_tensor(a, y0, -0.5, ve, ALU.mult, ALU.mult))
                step(V.tensor_tensor(b_, a, y0, ALU.mult))
                step(V.scalar_tensor_tensor(dst, b_, 1.5, y0, ALU.add, ALU.mult))

            def stats(step, src, st6, mv):
                step(*[V.bn_stats(st6[:, t, :], src(t)) for t in range(T)])
                V.memset(pad[:, :], 0.0)
                step(*[V.bn_aggr(mv[:, t, :], st6[:, t, :]) for t in range(T)])

            def normalise(step, dst, src, mv, r):
                step(*[V.tensor_scalar(dst[:, t, :], src(t), mv[:, t, 0:1], r[:, t:t + 1],
                                       ALU.subtract, ALU.mult) for t in range(T)])

            def g_part(s, part):
                step, skip = chain(g_vec, s, KG)
                skip((0, 4, 10, 14, 20)[part])
                if part == 0:
                    dve.wait_ge(x_loaded, 16 * (s + 1))
                    stats(step, lambda t: xin[:, t, :], gst, gmv)
                elif part == 1:
                    refine(step, (g_act, s * KGA + 2), gve[:, :], gy[:, :], gu[:, :], gw[:, :], gr[:, :],
                           gmv[:, :, 1], LN_EPS)
                    normalise(step, xn, lambda t: xin[:, t, :], gmv, gr)
                elif part == 2:
                    stats(step, lambda t: xn[:, t, :], gst, gmv)
                elif part == 3:
                    refine(step, (g_act, s * KGA + 4), gve[:, :], gy[:, :], gu[:, :], gw[:, :], gr[:, :],
                           gmv[:, :, 1], LN_EPS)
                    normalise(step, z, lambda t: xn[:, t, :], gmv, gr)
                else:
                    dve.wait_ge(g_tr, s + 1)
                    step(V.tensor_copy(xnT[:, 1:SEQ + 1], misc_b[0][:, 0:SEQ]),
                         V.tensor_scalar(hT[:, :], misc_b[0][:, SEQ:2 * SEQ], lng, lnb, ALU.mult, ALU.add))
                    step(V.tensor_copy(hTh[:, :], hT[:, :]))
                    step(V.tensor_tensor(hTl[:, :], hT[:, :], hTh[:, :], ALU.subtract))

            def qk_part(s, j):
                t, w = divmod(j, 4)
                dve.wait_ge(qk_sq, s * NJ + j + 1)
                V.tensor_reduce(ssq[:, j * 8:(j + 1) * 8], sq[:, j % 2, :].rearrange("p (h d) -> p h d", d=DH),
                                AX.X, ALU.add).then_inc(qk_sum, 1)
                if w < 2:
                    n = 2 * t + w
                    from_one(dve, q_lo, s * 2 * T + n - 1)
                    V.tensor_tensor(qc[:, n % 2, :], raw[:, j, :], crow[:, w * 512:(w + 1) * 512], ALU.mult
                                    ).then_inc(qc_done, 1)
                    dve.wait_ge(qc_done, s * 2 * T + n + 1)
                    V.tensor_copy(Qs[:, t, 4 * w:4 * w + 4, 0:4:3, :],
                                  qc[:, n % 2, :].rearrange("p (a h d) -> p a h d", h=2, d=DH)).then_inc(q_hi, 1)

            def norms(s):
                step, _ = chain(n_vec, s, KN)
                dve.wait_ge(qk_sum, (s + 1) * NJ)
                refine(step, (n_act, s * 2 + 2), nve[:, :], ny[:, :], nu[:, :], nw[:, :], nr[:, :],
                       ssq[:, :], L2_EPS * WS * WS)

            def scale_q(s):
                V.tensor_scalar(rq10[:, :, :], nr[:, :].rearrange("p (t w h) -> p t w h", t=T, w=2)[:, :, 0, :],
                                QK_SCALE * WS, None, ALU.mult).then_inc(n_vec, 1)

            def k_high(s, t):
                for n in (2 * t, 2 * t + 1):
                    t, w = divmod(n, 2)
                    dve.wait_ge(k_norm, s * 2 * T + n + 1)
                    V.tensor_copy(Kh[:, t, w * 8:(w + 1) * 8, :, :],
                                  raw[:, 4 * t + 2 + w, :].rearrange("p (h d) -> p h d", d=DH).unsqueeze(2)
                                  .broadcast_to([P, 8, 2, DH])).then_inc(k_hi, 1)

            def v_low(s, j):
                t, w = divmod(j, 2)
                dve.wait_ge(v_hi, s * 2 * T + j + 1)
                V.scalar_tensor_tensor(Vl[:, t, w * 512:(w + 1) * 512], misc_b[j % 2][:, :], 1.0 / WS,
                                       Vh[:, t, w * 512:(w + 1) * 512], ALU.mult, ALU.subtract
                                       ).then_inc(v_lo, 1)

            def copy_turned(s, n):
                dve.wait_ge(t_ready, s * NT + n + 1)
                dst, src = turned(n)
                V.tensor_copy(dst, src).then_inc(t_even, 1)

            def maxima(s, h):
                dve.wait_ge(sc_ready, s * H + h + 1)
                for t in range(T):
                    V.tensor_reduce(mx[:, h % 2, t:t + 1], score_b[h % 2][:, t * P:t * P + (t + 1) * P], AX.X,
                                    ALU.max, negate=True).then_inc(mx_done, 1)
                dve.wait_ge(mx_done, s * H * T + (h + 1) * T)
                if h == 0:
                    dve.wait_ge(n_vec, (s + 1) * KN)
                V.tensor_tensor(nb[:, h % 2, :], mx[:, h % 2, :], rq10[:, :, h], ALU.mult).then_inc(nb_done, 1)

            def p_high(s, h):
                dve.wait_ge(ex_done, s * 2 * H + 2 * h + 2)
                from_one(dve, pt_ready, s * H + h - 1)
                V.tensor_copy(Ph[:, h % 2, :], P32[:, h % 3, :]).then_inc(p_hi, 1)

            def copy_pt(s, h):
                dve.wait_ge(pt_ready, s * H + h + 1)
                from_one(dve, pv_done, s * H + h - 1)
                V.tensor_copy(PT[:, h % 2, :, :, :].rearrange("p a b q -> p (a b q)"),
                              turn_b[h % 2][:, :].bitcast(F16)[:, 0:6 * P]).then_inc(pt_even, 1)

            def divide(s, g):
                dve.wait_ge(ex_done, s * 2 * H + 2 * GH * (g + 1))
                V.reciprocal(rr[:, g % 2, :], rs[:, g, :, :].rearrange("p t h -> p (t h)")).then_inc(rr_done, 1)
                dve.wait_ge(rr_done, s * NG + g + 1)
                dve.wait_ge(pv_done, s * H + GH * (g + 1))
                V.tensor_tensor(On[:, g % 2, :, :].rearrange("p t (h d) -> p (t h) d", d=DH),
                                sum_b[g % 2][:, :].rearrange("p (a d) -> p a d", d=DH),
                                rr[:, g % 2, :].unsqueeze(2).broadcast_to([P, T * GH, DH]), ALU.mult
                                ).then_inc(on_done, 1)

            def o_part(s, part):
                step, skip = chain(o_vec, s, KO)
                skip((0, 4, 10, 13, 17, 20)[part])
                o0, o1 = misc_b
                src = lambda t: o0[:, t * P:(t + 1) * P]
                if part == 0:
                    dve.wait_ge(wo_ready, s + 1)
                    stats(step, src, ost, omv)
                elif part == 1:
                    refine(step, (o_act, s * KOA + 2), ove[:, :], oy[:, :], ou[:, :], ow[:, :], orr[:, :],
                           omv[:, :, 1], LN_EPS)
                    normalise(step, z2, src, omv, orr)
                elif part == 2:
                    dve.wait_ge(o_tr, s + 1)
                    step(V.tensor_scalar(h2T[:, :], o1[:, 0:SEQ], lng, lnb, ALU.mult, ALU.add))
                    step(V.tensor_copy(h2h[:, :], h2T[:, :]))
                    step(V.tensor_tensor(h2l[:, :], h2T[:, :], h2h[:, :], ALU.subtract))
                elif part == 3:
                    dve.wait_ge(o_gate, s + 1)
                    step(V.tensor_tensor(gl[:, :, :], o0[:, 0:T * NE].rearrange("p (t e) -> p t e", t=T),
                                         gbrow[:, :].unsqueeze(1).broadcast_to([P, T, NE]), ALU.add))
                    step(V.tensor_reduce(gm[:, :], gl[:, :, :], AX.X, ALU.max))
                    step(*[V.tensor_scalar(gl[:, t, :], gl[:, t, :], gm[:, t:t + 1], None, ALU.subtract)
                           for t in range(T)])
                elif part == 4:
                    dve.wait_ge(o_act, (s + 1) * KOA)
                    step(V.reciprocal(grs[:, :], gs[:, :]))
                    step(*[V.tensor_scalar(gate[:, t, 0:NE], ge[:, t, :], grs[:, t:t + 1], None, ALU.mult)
                           for t in range(T)])
                else:
                    dve.wait_ge(o_gT, s + 1)
                    step(V.tensor_copy(gateT[:, :], o1[:, 0:SEQ]))
                    dve.wait_ge(o_b2, s + 1)
                    step(V.tensor_copy(acc[:, :, :].rearrange("p t d -> p (t d)"), o0[:, 0:SEQ]))

            def add_expert(s, e):
                dve.wait_ge(w2_ready, s * NE * T + (e + 1) * T)
                for t in range(T):
                    if e > 0:
                        dve.wait_ge(acc_done, s * NE * T + (e - 1) * T + t + 1)
                    V.scalar_tensor_tensor(acc[:, t, :], sum_b[e % 2][:, t * P:(t + 1) * P],
                                           gate[:, t, e:e + 1], acc[:, t, :], ALU.mult, ALU.add
                                           ).then_inc(acc_done, 1)

            def convolve(s):
                step, _ = chain(c_vec, s, KC)
                step(V.tensor_scalar(cv[:, 0, :], xnT[:, 1:SEQ + 1], cols[:, 5:6], cb, ALU.mult, ALU.add))
                step(V.scalar_tensor_tensor(cv[:, 1, :], xnT[:, 0:SEQ], cols[:, 4:5], cv[:, 0, :],
                                            ALU.mult, ALU.add))
                step(V.scalar_tensor_tensor(xf[:, :], xnT[:, 2:SEQ + 2], cols[:, 6:7], cv[:, 1, :],
                                            ALU.mult, ALU.add))

            def step_inputs(s):
                step, skip = chain(c_vec, s, KC)
                skip(3)
                dve.wait_ge(tanh_done, s + 1)
                half = 0.5 * (DT_MAX - DT_MIN)
                step(V.tensor_scalar(dt[:, :], th[:, :], half, half + DT_MIN, ALU.mult, ALU.add))
                step(V.tensor_tensor(u[:, :], dt[:, :], xf[:, :], ALU.mult))

            def scan(s, d):
                dve.wait_ge(a_done, s * DS + d + 1)
                V.tensor_tensor_scan(st[:, d % 2, :], aexp[:, d, :], u[:, :], 0.0, ALU.mult, ALU.add
                                     ).then_inc(scan_done, 1)
                dve.wait_ge(scan_done, s * DS + d + 1)
                if d == 0:
                    V.tensor_scalar(y[:, :], st[:, 0, :], bc[:, 0:1], None, ALU.mult).then_inc(y_done, 1)
                else:
                    dve.wait_ge(y_done, s * DS + d)
                    V.scalar_tensor_tensor(y[:, :], st[:, d % 2, :], bc[:, d:d + 1], y[:, :],
                                           ALU.mult, ALU.add).then_inc(y_done, 1)

            def e_part(s, part):
                step, skip = chain(e_vec, s, KE)
                skip((0, 4)[part])
                if part == 0:
                    dve.wait_ge(acc_done, (s + 1) * NE * T)
                    stats(step, lambda t: acc[:, t, :], est, emv)
                    return
                refine(step, (e_act, s * 2 + 2), eve[:, :], ey[:, :], eu[:, :], ew[:, :], er[:, :],
                       emv[:, :, 1], LN_EPS)
                normalise(step, e1, lambda t: acc[:, t, :], emv, er)
                step(V.tensor_tensor(e2[:, :, :], e1[:, :, :], grow[:, :].unsqueeze(1).broadcast_to([P, T, D]),
                                     ALU.mult))
                dve.wait_ge(fin_free, 16 * (s + 1))
                step(V.tensor_tensor(fin[:, :, :], e2[:, :, :], xy[:, :, :], ALU.add))

            def add_y(s):
                dve.wait_ge(xb_done, s + 1)
                dve.wait_ge(y_tr, s + 1)
                V.tensor_tensor(xy[:, :, :].rearrange("p t d -> p (t d)"), misc_b[1][:, 0:SEQ],
                                xb[:, :, :].rearrange("p t d -> p (t d)"), ALU.add).then_inc(xy_done, 1)

            def prologue():
                V.memset(pad[:, :], 0.0).then_inc(fin_free, 16)
                V.memset(eps_ln[:, :], LN_EPS)
                V.memset(eps_l2[:, :], L2_EPS * WS * WS)
                V.memset(xnT[:, :], 0.0)
                V.memset(gate[:, :, :].rearrange("p t e -> p (t e)"), 0.0)
                dve.wait_ge(const_pool, 4)
                V.tensor_copy(ident16[:, :], ident[:, :]).then_inc(const_vec, 1)
                V.tensor_copy(identb[:, :], ident[:, :]).then_inc(const_vec, 1)
                V.tensor_copy(maskb[:, :], mask[:, :]).then_inc(const_vec, 1)
                g_part(0, 0)
                g_part(0, 1)
                g_part(0, 2)
                g_part(0, 3)
                dve.wait_ge(w_high, 1)
                V.scalar_tensor_tensor(wl[:, :], W32, WS, wh[:, :], ALU.mult, ALU.subtract).then_inc(w_low, 1)
                dve.wait_ge(setup_tr, 1)
                dve.wait_ge(d_small, 16 * 17)
                V.tensor_copy(dtwT[:, :], misc_b[1][:, 0:D])
                V.tensor_copy(b1c[:, :], misc_b[1][:, D:D + NE * FC]).then_inc(setup_vec, 1)
                V.tensor_scalar(half_dtb[:, :], dtb, 0.5, None, ALU.mult)
                V.tensor_tensor(bc[:, :], bs[:, :], cs[:, :], ALU.mult)
                V.scalar_tensor_tensor(crow[:, :], crow[:, :], 1.0 / WS, krow, ALU.mult, ALU.mult
                                       ).then_inc(setup_vec, 1)
                dve.wait_ge(setup_vec, 2)
                g_part(0, 4)
                for j in range(NJ):
                    qk_part(0, j)
                dve.wait_ge(setup_act, 3)
                V.scalar_tensor_tensor(spt[:, 3, :], al[:, :], 0.0, spt[:, 2, :], ALU.max, ALU.add
                                       ).then_inc(setup_vec, 1)
                dve.wait_ge(setup_vec, 3)
                V.tensor_scalar(negA[:, :], spt[:, 3, :], -1.0, None, ALU.mult).then_inc(setup_vec, 1)
                norms(0)
                scale_q(0)
                for j in range(2 * T):
                    v_low(0, j)
                k_high(0, 0)
                k_high(0, 1)
                for n in range(0, NT, 2):
                    copy_turned(0, n)
                convolve(0)
                for part in range(5):
                    g_part(1, part)
                dve.wait_ge(w1_high, 1)
                V.scalar_tensor_tensor(w1l[:, :], W132, WS, w1h[:, :], ALU.mult, ALU.subtract
                                       ).then_inc(w1_low, 1)

            def heads(i, k):
                if 1 <= k < H + 1:
                    maxima(i, k - 1)
                if 2 <= k < H + 2:
                    p_high(i, k - 2)
                if 4 <= k < H + 4 and k % 2 == 0:
                    copy_pt(i, k - 4)
                if k >= 9 and k % GH == 1 and k < 9 + 4 * NG:
                    divide(i, (k - 9) // GH)

            def body(i, older, old, new, newer):
                for k in range(H + 1):
                    if k == 0:
                        step_inputs(i)
                    heads(i, k)
                    if older and k in (0, 1):
                        e_part(i - 2, k)
                    if old and k == 1:
                        add_y(i - 1)
                    if new and 4 <= k < 4 + NJ:
                        qk_part(i + 1, k - 4)
                    if newer and k in (9, 11, 12, 14):
                        g_part(i + 2, (9, 11, 12, 14).index(k))
                    if old and k in (10, 12, 14, 16):
                        o_part(i - 1, (10, 12, 14, 16).index(k))
                    if new and k == 13:
                        norms(i + 1)
                    if new and k in (15, 16):
                        k_high(i + 1, k - 15)
                for m in range(NE + 2):
                    for k in (H + 1 + 2 * m, H + 2 + 2 * m):
                        heads(i, k)
                    if old and m in (0, 1):
                        o_part(i - 1, 4 + m)
                    if new and m == 1:
                        scale_q(i + 1)
                    if old and m >= 2:
                        add_expert(i - 1, m - 2)
                    if new and 3 <= m < 8:
                        copy_turned(i + 1, 2 * m - 6)
                    if new and m in (3, 5):
                        v_low(i + 1, m - 3)
                        v_low(i + 1, m - 2)
                    if new and m == 5:
                        convolve(i + 1)
                    if newer and m == 7:
                        g_part(i + 2, 4)
                    if m < NE:
                        scan(i, 2 * m)
                        scan(i, 2 * m + 1)

            def tail():
                e_part(LAST - 1, 0)
                e_part(LAST - 1, 1)
                add_y(LAST)
                for part in range(6):
                    o_part(LAST, part)
                for e in range(NE):
                    add_expert(LAST, e)
                e_part(LAST, 0)
                e_part(LAST, 1)

            bodies(dve, prologue, body, tail)


_INS = ['x', 'a_log', 'b', 'c', 'dt_w', 'dt_b', 'conv_w', 'conv_b']
_FFN = ['ln_g', 'ln_b', 'Wq', 'Wk', 'Wv', 'q_scale', 'k_scale', 'Wo', 'gate_w', 'gate_b', 'w1', 'b1', 'w2', 'b2']


def kernel(**inputs):
    import concourse.bacc as bacc
    from concourse.bass_utils import run_bass_kernel_spmd

    nc = bacc.Bacc("TRN2", target_bir_lowering=False, num_devices=1)
    arrays, args = {}, []
    for name in [f"L0_attn_{n}" for n in _INS] + [f"L0_ffn_{n}" for n in _FFN]:
        a = np.ascontiguousarray(inputs[name])
        arrays[f"in_{name}"] = a
        args.append(nc.dram_tensor(f"in_{name}", a.shape, mybir.dt.from_np(a.dtype), kind="ExternalInput").ap())
    shape = inputs["L0_attn_x"].shape
    args.append(nc.dram_tensor("out_dram", shape, F32, kind="ExternalOutput").ap())
    build(nc, *args)
    r = run_bass_kernel_spmd(nc, [arrays], core_ids=[0])
    return r.results[0]["out_dram"]
```

```python
from contextlib import ExitStack

import numpy as np
import concourse.bass as bass
from concourse import mybir
from concourse.alu_op_type import AluOpType as ALU

F32 = mybir.dt.float32
F16 = mybir.dt.float16
BF16 = mybir.dt.bfloat16
ACT = mybir.ActivationFunctionType
AX = mybir.AxisListType

NSEQ, SEQ, D = 16, 256, 128
P = 128
T = SEQ // P
H, DH = 16, 64
HD = H * DH
NE, FF = 8, 512
FC = FF // P
DS = 16
GH = 4
NG = H // GH
PC = SEQ + P
NJ = 4 * T
NT = 5 * T
WS = 64.0
LN_EPS, L2_EPS = 1e-5, 1e-12
QK_SCALE = 10.0
DT_MIN, DT_MAX = 0.001, 0.1
MASKED = -1e9
LAST = NSEQ - 1

KG, KGA = 24, 4
KN = 5
KO, KOA = 22, 4
KE = 12
KC = 5


def build(nc, x, a_log, b, c, dt_w, dt_b, conv_w, conv_b, ln_g, ln_b, Wq, Wk, Wv, q_scale, k_scale,
          Wo, gate_w, gate_b, w1, b1, w2, b2, out):
    ctx = ExitStack()
    with ctx:
        def sb(name, shape, dt=F32):
            return ctx.enter_context(nc.sbuf_tensor(name, shape, dt))

        def sem(name):
            return ctx.enter_context(nc.semaphore(name))

        ident = sb("ident", [P, P])
        ident16 = sb("ident16", [P, P], F16)
        identb = sb("identb", [P, P], BF16)
        mask = sb("mask", [P, P])
        maskb = sb("maskb", [P, P], BF16)
        wh = sb("wh", [P, 3 * HD], F16)
        wl = sb("wl", [P, 3 * HD], F16)
        w1h = sb("w1h", [P, NE * FF], F16)
        w1l = sb("w1l", [P, NE * FF], F16)
        w2s = sb("w2s", [P, NE * FC, D])
        wos = sb("wos", [P, HD // P, D])
        crow = sb("crow", [P, HD])
        dtw = sb("dtw", [P, D])
        dtwT = sb("dtwT", [P, D])
        b1r = sb("b1r", [NE * FC, P])
        b1c = sb("b1c", [P, NE * FC])
        cols = sb("cols", [P, 8])
        lng, lnb, dtb, cb = (cols[:, n:n + 1] for n in range(4))
        half_dtb = sb("half_dtb", [P, 1])
        grow = sb("grow", [P, D])
        brow = sb("brow", [P, D])
        gbrow = sb("gbrow", [P, NE])
        gws = sb("gws", [P, NE])
        b2s = sb("b2s", [NE, D])
        al = sb("al", [P, DS])
        bs = sb("bs", [P, DS])
        cs = sb("cs", [P, DS])
        bc = sb("bc", [P, DS])
        spt = sb("spt", [P, 4, DS])
        negA = sb("negA", [P, DS])
        eps_ln = sb("eps_ln", [P, 1])
        eps_l2 = sb("eps_l2", [P, 1])
        pad = sb("pad", [P, 1])
        xin = sb("xin", [P, T, D])
        xn = sb("xn", [P, T, D])
        z = sb("z", [P, T, D])
        gst = sb("gst", [P, T, 6])
        gmv = sb("gmv", [P, T, 2])
        gve = sb("gve", [P, T])
        gln = sb("gln", [P, T])
        gy = sb("gy", [P, T])
        gu = sb("gu", [P, T])
        gw = sb("gw", [P, T])
        gr = sb("gr", [P, T])
        xnT = sb("xnT", [P, SEQ + 2])
        hT = sb("hT", [P, SEQ])
        hTh = sb("hTh", [P, SEQ], F16)
        hTl = sb("hTl", [P, SEQ], F16)
        raw = sb("raw", [P, NJ, 512])
        sq = sb("sq", [P, 2, 512])
        ssq = sb("ssq", [P, NJ * 8])
        nve = sb("nve", [P, NJ * 8])
        nln = sb("nln", [P, NJ * 8])
        ny = sb("ny", [P, NJ * 8])
        nu = sb("nu", [P, NJ * 8])
        nw = sb("nw", [P, NJ * 8])
        nr = sb("nr", [P, NJ * 8])
        rq10 = sb("rq10", [P, T, H])
        qc = sb("qc", [P, 2, 512])
        Qs = sb("Qs", [P, T, H // 2, 4, DH], F16)
        Kh = sb("Kh", [P, T, H, 2, DH], F16)
        Kl = sb("Kl", [P, T, HD], F16)
        QT = sb("QT", [P, H, SEQ], F16)
        KT = sb("KT", [P, H, SEQ], F16)
        KL = sb("KL", [P, H // 2, SEQ], F16)
        Vh = sb("Vh", [P, T, HD], F16)
        Vl = sb("Vl", [P, T, HD], F16)
        mx = sb("mx", [P, 2, T])
        nb = sb("nb", [P, 2, T])
        P32 = sb("P32", [P, 3, PC])
        Ph = sb("Ph", [P, 2, PC], F16)
        Pl = sb("Pl", [P, 2, PC], F16)
        PT = sb("PT", [P, 2, 2, 3, P], F16)
        rs = sb("rs", [P, NG, T, GH])
        rr = sb("rr", [P, 2, T * GH])
        On = sb("On", [P, 2, T, GH * DH])
        OT = sb("OT", [P, HD // P, SEQ])
        ost = sb("ost", [P, T, 6])
        omv = sb("omv", [P, T, 2])
        ove = sb("ove", [P, T])
        oln = sb("oln", [P, T])
        oy = sb("oy", [P, T])
        ou = sb("ou", [P, T])
        ow = sb("ow", [P, T])
        orr = sb("orr", [P, T])
        z2 = sb("z2", [P, T, D])
        h2T = sb("h2T", [P, SEQ])
        h2h = sb("h2h", [P, SEQ], F16)
        h2l = sb("h2l", [P, SEQ], F16)
        gl = sb("gl", [P, T, NE])
        gm = sb("gm", [P, T])
        ge = sb("ge", [P, T, NE])
        gs = sb("gs", [P, T])
        grs = sb("grs", [P, T])
        gate = sb("gate", [P, T, P])
        gateT = sb("gateT", [P, SEQ])
        hid = sb("hid", [P, 2, FC, SEQ])
        acc = sb("acc", [P, T, D])
        aexp = sb("aexp", [P, DS, SEQ])
        xf = sb("xf", [P, SEQ])
        cv = sb("cv", [P, 2, SEQ])
        th = sb("th", [P, SEQ])
        dt = sb("dt", [P, SEQ])
        u = sb("u", [P, SEQ])
        st = sb("st", [P, 2, SEQ])
        y = sb("y", [P, SEQ])
        est = sb("est", [P, T, 6])
        emv = sb("emv", [P, T, 2])
        eve = sb("eve", [P, T])
        eln = sb("eln", [P, T])
        ey = sb("ey", [P, T])
        eu = sb("eu", [P, T])
        ew = sb("ew", [P, T])
        er = sb("er", [P, T])
        e1 = sb("e1", [P, T, D])
        e2 = sb("e2", [P, T, D])
        xy = sb("xy", [P, T, D])
        fin = sb("fin", [P, T, D])
        xres = sb("xres", [P, T, D])
        xb = sb("xb", [P, T, D])
        krow = sq[:, :, :].rearrange("p a n -> p (a n)")
        W32 = raw[:, 0:6, :].rearrange("p a n -> p (a n)")
        W132 = aexp[:, :, :].rearrange("p a n -> p (a n)")

        bank = [ctx.enter_context(nc.psum_tensor(f"bank{n}", [P, 512], F32)) for n in range(8)]
        score_b = bank[0:2]
        turn_b = bank[2:4]
        sum_b = bank[4:6]
        misc_b = bank[6:8]

        names = """d_small d_w d_w1 d_w2 d_wo d_rows x_loaded xres_loaded fin_free
            const_pool const_vec w_high w_low w1_high w1_low setup_tr setup_vec setup_act
            g_vec g_act g_tr
            qk_ready qk_raw qk_sq qk_sum qc_done q_hi q_lo n_vec n_act k_norm k_hi k_lo
            v_ready v_hi v_lo t_ready t_even t_odd
            sc_ready mx_done nb_done ex_done p_hi p_lo pt_ready pt_even pt_odd pv_done rr_done on_done
            ot_ready ot_done
            wo_ready o_vec o_act o_tr o_gate o_gT o_b2
            w1_ready gelu_done w2_ready acc_done
            c_vec dt_ready tanh_done a_done scan_done y_done
            y_tr e_vec e_act xb_done xy_done""".split()
        S = {n: sem(n) for n in names}
        (d_small, d_w, d_w1, d_w2, d_wo, d_rows, x_loaded, xres_loaded, fin_free,
         const_pool, const_vec, w_high, w_low, w1_high, w1_low, setup_tr, setup_vec, setup_act,
         g_vec, g_act, g_tr,
         qk_ready, qk_raw, qk_sq, qk_sum, qc_done, q_hi, q_lo, n_vec, n_act, k_norm, k_hi, k_lo,
         v_ready, v_hi, v_lo, t_ready, t_even, t_odd,
         sc_ready, mx_done, nb_done, ex_done, p_hi, p_lo, pt_ready, pt_even, pt_odd, pv_done, rr_done, on_done,
         ot_ready, ot_done,
         wo_ready, o_vec, o_act, o_tr, o_gate, o_gT, o_b2,
         w1_ready, gelu_done, w2_ready, acc_done,
         c_vec, dt_ready, tanh_done, a_done, scan_done, y_done,
         y_tr, e_vec, e_act, xb_done, xy_done) = (S[n] for n in names)

        def tiles(ap):
            return ap.rearrange("(t p) d -> p t d", p=P)

        def turned(n):
            src = turn_b[n % 2][:, :].bitcast(F16).rearrange("p (m q) -> p m q", q=P)
            if n < 8:
                t, h = (n % 4) // 2, (n % 2) * 8
                return (QT, KT)[n // 4][:, h:h + 8, t * P:(t + 1) * P], src
            return KL[:, :, (n - 8) * P:(n - 7) * P], src

        def bodies(eng, prologue, body, tail):
            prologue()
            body(0, older=False, old=False, new=True, newer=True)
            body(1, older=False, old=True, new=True, newer=True)
            with eng.Fori(2, NSEQ - 2) as i:
                body(i, older=True, old=True, new=True, newer=True)
            body(NSEQ - 2, older=True, old=True, new=True, newer=False)
            body(LAST, older=True, old=True, new=False, newer=False)
            tail()

        def from_one(eng, semaphore, value):
            if not isinstance(value, int) or value > 0:
                eng.wait_ge(semaphore, value)

        block = ctx.enter_context(nc.Block())

        @block.sync
        def _(sp):
            def load_x(s):
                if not isinstance(s, int) or s > 0:
                    sp.wait_ge(g_vec, (s - 1) * KG + 10)
                sp.dma_start(xin[:, :, :], tiles(x[s])).then_inc(x_loaded, 16)

            def load_xres(s):
                if not isinstance(s, int) or s > 0:
                    sp.wait_ge(xb_done, s)
                sp.dma_start(xres[:, :, :], tiles(x[s])).then_inc(xres_loaded, 16)

            def store_out(s):
                sp.wait_ge(e_vec, (s + 1) * KE)
                sp.dma_start(tiles(out[s]), fin[:, :, :]).then_inc(fin_free, 16)

            def prologue():
                load_x(0)
                load_xres(0)
                for n, w in enumerate((Wq, Wk, Wv)):
                    sp.dma_start(W32[:, n * HD:(n + 1) * HD], w).then_inc(d_w, 16)
                load_x(1)
                sp.dma_start(W132.rearrange("p (e f) -> p e f", e=NE),
                             w1.rearrange("e p f -> p e f")).then_inc(d_w1, 16)
                sp.dma_start(w2s[:, :, :].rearrange("p (e c) n -> p e c n", e=NE),
                             w2.rearrange("e (c p) n -> p e c n", p=P)).then_inc(d_w2, 16)

            def body(i, older, old, new, newer):
                if newer:
                    load_x(i + 2)
                if old:
                    load_xres(i)
                if older:
                    store_out(i - 2)

            def tail():
                store_out(LAST - 1)
                store_out(LAST)
                sp.wait_ge(fin_free, 16 * (NSEQ + 1))

            bodies(sp, prologue, body, tail)

        @block.tensor
        def _(pe):
            mm, tr = nc.tensor.matmul, nc.tensor.transpose

            def turn(s):
                pe.wait_ge(g_vec, s * KG + 20)
                for t in range(T):
                    tr(misc_b[0][:, t * P:(t + 1) * P], xn[:, t, :], ident[:, :])
                for t in range(T):
                    last = tr(misc_b[0][:, SEQ + t * P:SEQ + (t + 1) * P], z[:, t, :], ident[:, :])
                last.then_inc(g_tr, 1)

            def split(dst, s, t, w0, ready):
                hi, lo = hTh[:, t * P:(t + 1) * P], hTl[:, t * P:(t + 1) * P]
                mm(dst, hi, wh[:, w0:w0 + 512], start=True, stop=False)
                mm(dst, lo, wh[:, w0:w0 + 512], start=False, stop=False)
                mm(dst, hi, wl[:, w0:w0 + 512], start=False, stop=True).then_inc(ready, 1)

            def project(s, j):
                if j == 0:
                    pe.wait_ge(g_vec, (s + 1) * KG)
                if j >= 2:
                    pe.wait_ge(qk_raw, s * NJ + j - 1)
                t, w = divmod(j, 4)
                split(misc_b[j % 2][:, :], s, t, w * 512, qk_ready)

            def project_v(s, j):
                if j == 0:
                    pe.wait_ge(qk_raw, (s + 1) * NJ)
                    from_one(pe, o_vec, (s - 1) * KO)
                if j >= 2:
                    pe.wait_ge(v_lo, s * 2 * T + j - 1)
                t, w = divmod(j, 2)
                split(misc_b[j % 2][:, :], s, t, 2 * HD + w * 512, v_ready)

            def turn_qk(s, n):
                if n == 0:
                    pe.wait_ge(q_lo, (s + 1) * 2 * T)
                if n == 4:
                    pe.wait_ge(k_lo, (s + 1) * 2 * T)
                if n >= 2:
                    pe.wait_ge((t_even, t_odd)[n % 2], s * (NT // 2) + n // 2)
                dst = turn_b[n % 2][:, :].bitcast(F16)
                for m in range(8):
                    if n < 8:
                        t, h = (n % 4) // 2, (n % 2) * 8 + m
                    if n < 4:
                        src = Qs[:, t, h // 2, 2 * (h % 2):2 * (h % 2) + 2, :].rearrange("p a d -> p (a d)")
                    elif n < 8:
                        src = Kh[:, t, h, :, :].rearrange("p a d -> p (a d)")
                    else:
                        src = Kl[:, n - 8, m * P:(m + 1) * P]
                    last = tr(dst[:, m * P:(m + 1) * P], src, ident16[:, :])
                last.then_inc(t_ready, 1)

            def scores(s, h, before):
                if h == 0:
                    pe.wait_ge(t_even, (s + 1) * (NT // 2))
                    pe.wait_ge(t_odd, (s + 1) * (NT // 2))
                    if before:
                        pe.wait_ge(gelu_done, (s - 1) * NE * FC)
                if h >= 2:
                    pe.wait_ge(ex_done, s * 2 * H + 2 * (h - 1))
                o, p0 = score_b[h % 2], DH * (h % 2)
                for t in range(T):
                    keys = (t + 1) * P
                    dst = o[:, t * P:t * P + keys]
                    q = QT[:, h, t * P:(t + 1) * P]
                    mm(dst, q, KT[:, h, 0:keys], start=True, stop=False)
                    mm(dst, q[p0:p0 + DH, :], KL[p0:p0 + DH, h // 2, 0:keys], start=False, stop=False)
                    last = mm(dst[:, t * P:keys], identb[:, :], maskb[:, :], start=False, stop=True)
                last.then_inc(sc_ready, 1)

            def turn_p(s, h):
                pe.wait_ge(p_lo, s * H + h + 1)
                dst = turn_b[h % 2][:, :].bitcast(F16)
                for n, src in enumerate((Ph, Pl)):
                    for m in range(3):
                        last = tr(dst[:, (3 * n + m) * P:(3 * n + m + 1) * P],
                                  src[:, h % 2, m * P:(m + 1) * P], ident16[:, :])
                last.then_inc(pt_ready, 1)

            def weigh(s, h, before):
                g = h // GH
                pe.wait_ge((pt_even, pt_odd)[h % 2], s * (H // 2) + h // 2 + 1)
                if h == 0:
                    pe.wait_ge(v_lo, (s + 1) * 2 * T)
                    if before:
                        pe.wait_ge(acc_done, (s - 1) * NE * T)
                if h % GH == 0 and g >= 2:
                    pe.wait_ge(ot_done, s * NG + g - 1)
                for t in range(T):
                    dst = sum_b[g % 2][:, (t * GH + h % GH) * DH:(t * GH + h % GH + 1) * DH]
                    terms = [(a, kb) for kb in range(t + 1) for a in ((0, Vh), (0, Vl), (1, Vh))]
                    for n, ((half, v), kb) in enumerate(terms):
                        last = mm(dst, PT[:, h % 2, half, t + kb, :], v[:, kb, h * DH:(h + 1) * DH],
                                  start=(n == 0), stop=(n == len(terms) - 1))
                last.then_inc(pv_done, 1)

            def turn_o(s, g):
                pe.wait_ge(on_done, s * NG + g + 1)
                for m in range(2):
                    for t in range(T):
                        last = tr(sum_b[g % 2][:, (m * T + t) * P:(m * T + t + 1) * P],
                                  On[:, g % 2, t, m * P:(m + 1) * P], ident[:, :])
                last.then_inc(ot_ready, 1)

            def output(s, part):
                o0, o1 = misc_b
                if part < T:
                    t = part
                    if t == 0:
                        pe.wait_ge(ot_done, (s + 1) * NG)
                    for m in range(HD // P):
                        last = mm(o0[:, t * P:(t + 1) * P], OT[:, m, t * P:(t + 1) * P],
                                  wos[:, m, :], start=(m == 0), stop=(m == HD // P - 1))
                    if t == T - 1:
                        last.then_inc(wo_ready, 1)
                elif part == 2:
                    pe.wait_ge(o_vec, s * KO + 10)
                    for t in range(T):
                        last = tr(o1[:, t * P:(t + 1) * P], z2[:, t, :], ident[:, :])
                    last.then_inc(o_tr, 1)
                elif part == 3:
                    pe.wait_ge(o_vec, s * KO + 11)
                    for t in range(T):
                        last = mm(o0[:, t * NE:(t + 1) * NE], h2T[:, t * P:(t + 1) * P], gws[:, :],
                                  start=True, stop=True)
                    last.then_inc(o_gate, 1)
                elif part == 4:
                    pe.wait_ge(o_vec, s * KO + 20)
                    for t in range(T):
                        last = tr(o1[:, t * P:(t + 1) * P], gate[:, t, :], ident[:, :])
                    last.then_inc(o_gT, 1)
                else:
                    pe.wait_ge(o_vec, s * KO + 21)
                    for t in range(T):
                        last = mm(o0[:, t * P:(t + 1) * P], gateT[0:NE, t * P:(t + 1) * P], b2s[:, :],
                                  start=True, stop=True)
                    last.then_inc(o_b2, 1)

            def expert_up(s, e):
                if e == 0:
                    pe.wait_ge(o_vec, s * KO + 13)
                for q in (2 * e, 2 * e + 1):
                    if q >= 2:
                        pe.wait_ge(gelu_done, s * NE * FC + 2 * (q - 1))
                    for m in range(2):
                        f = (2 * q + m) * P
                        dst = score_b[q % 2][:, m * SEQ:(m + 1) * SEQ]
                        mm(dst, w1h[:, f:f + P], h2h[:, :], start=True, stop=False)
                        mm(dst, w1h[:, f:f + P], h2l[:, :], start=False, stop=False)
                        last = mm(dst, w1l[:, f:f + P], h2h[:, :], start=False, stop=True)
                    last.then_inc(w1_ready, 1)

            def expert_down(s, e):
                pe.wait_ge(gelu_done, s * NE * FC + FC * (e + 1))
                if e >= 2:
                    pe.wait_ge(acc_done, s * NE * T + T * (e - 1))
                for t in range(T):
                    for m in range(FC):
                        last = mm(sum_b[e % 2][:, t * P:(t + 1) * P], hid[:, e % 2, m, t * P:(t + 1) * P],
                                  w2s[:, e * FC + m, :], start=(m == 0), stop=(m == FC - 1))
                    last.then_inc(w2_ready, 1)

            def step_sizes(s):
                pe.wait_ge(c_vec, s * KC + 3)
                pe.wait_ge(v_lo, (s + 1) * 2 * T)
                mm(misc_b[1][:, 0:SEQ], dtwT[:, :], xf[:, :], start=True, stop=True).then_inc(dt_ready, 1)

            def turn_y(s):
                pe.wait_ge(y_done, (s + 1) * DS)
                for t in range(T):
                    last = tr(misc_b[1][:, t * P:(t + 1) * P], y[:, t * P:(t + 1) * P], ident[:, :])
                last.then_inc(y_tr, 1)

            def heads(i, k, old, older):
                if k < H:
                    scores(i, k, older)
                if 5 <= k < H + 5:
                    weigh(i, k - 5, older)
                if 3 <= k < H + 3:
                    turn_p(i, k - 3)
                if k in (10, 14, 18):
                    turn_o(i, (k - 10) // GH)
                if k == 21:
                    turn_o(i, NG - 1)

            def prologue():
                pe.wait_ge(const_vec, 3)
                pe.wait_ge(d_small, 16 * 17)
                tr(misc_b[1][:, 0:D], dtw[:, :], ident[:, :])
                tr(misc_b[1][:, D:D + NE * FC], b1r[:, :], ident[0:NE * FC, 0:NE * FC]).then_inc(setup_tr, 1)
                turn(0)
                pe.wait_ge(w_low, 1)
                pe.wait_ge(setup_vec, 1)
                for j in range(NJ):
                    project(0, j)
                for j in range(2 * T):
                    project_v(0, j)
                for n in range(NT):
                    turn_qk(0, n)
                pe.wait_ge(v_lo, 2 * T)
                turn(1)
                step_sizes(0)
                pe.wait_ge(w1_low, 1)
                pe.wait_ge(d_w2, 16)
                pe.wait_ge(d_wo, 16)

            def body(i, older, old, new, newer):
                for k in range(H + 1):
                    heads(i, k, old, older)
                    if old and k == 0:
                        pe.wait_ge(tanh_done, i + 1)
                        turn_y(i - 1)
                    if new and 2 <= k < 2 + NJ:
                        if k == 3:
                            if old:
                                pe.wait_ge(xy_done, i)
                            else:
                                pe.wait_ge(tanh_done, i + 1)
                        project(i + 1, k - 2)
                    if old and k == 9:
                        if new:
                            pe.wait_ge(qk_raw, (i + 2) * NJ - 1)
                        output(i - 1, 0)
                    if old and k == 10:
                        output(i - 1, 1)
                    if old and k == 13:
                        if new:
                            pe.wait_ge(qk_raw, (i + 2) * NJ)
                        else:
                            pe.wait_ge(xy_done, i)
                        output(i - 1, 2)
                    if old and k == 15:
                        output(i - 1, 3)
                if old:
                    pe.wait_ge(ex_done, (i + 1) * 2 * H)
                for m in range(NE + 2):
                    for k in (H + 1 + 2 * m, H + 2 + 2 * m):
                        heads(i, k, old, older)
                        if old and k % 2 == 1 and m < NE:
                            expert_up(i - 1, m)
                    if old and m in (0, 1):
                        output(i - 1, 4 + m)
                    if old and 1 <= m <= NE:
                        if m <= 2:
                            pe.wait_ge(ot_done, i * NG + 2 + m)
                        expert_down(i - 1, m - 1)
                    if new and m in (2, 4):
                        project_v(i + 1, m - 2)
                        project_v(i + 1, m - 1)
                    if new and 2 <= m < 7:
                        turn_qk(i + 1, 2 * m - 4)
                        turn_qk(i + 1, 2 * m - 3)
                    if new and m == 6:
                        if newer:
                            pe.wait_ge(v_lo, (i + 2) * 2 * T)
                            turn(i + 2)
                        step_sizes(i + 1)

            def tail():
                pe.wait_ge(o_vec, LAST * KO)
                turn_y(LAST)
                output(LAST, 0)
                output(LAST, 1)
                pe.wait_ge(xy_done, NSEQ)
                for part in range(2, 4):
                    output(LAST, part)
                for e in range(NE + 1):
                    if e < NE:
                        expert_up(LAST, e)
                    if e < 2:
                        output(LAST, 4 + e)
                    if e >= 1:
                        expert_down(LAST, e - 1)

            bodies(pe, prologue, body, tail)

        @block.scalar
        def _(act):
            fn = nc.scalar.activation

            def with_exp_and_ln():
                nc.scalar.preload_act_table_set("natural_log_exp_and_others")

            def with_gelu_and_tanh():
                nc.scalar.preload_act_table_set("gelu_apprx_tanh_and_others")

            def inverse_root(semaphore, at, src, ln, dst, eps):
                fn(ln, src, ACT.Ln, bias=eps).then_inc(semaphore, 1)
                act.wait_ge(semaphore, at + 1)
                fn(dst, ln, ACT.Exp, scale=-0.5).then_inc(semaphore, 1)

            def norm(s, n):
                act.wait_ge(g_vec, s * KG + (4, 14)[n])
                inverse_root(g_act, s * KGA + 2 * n, gmv[:, :, 1], gln[:, :], gy[:, :], eps_ln[:, :])

            def copy_raw(s, j):
                act.wait_ge(qk_ready, s * NJ + j + 1)
                fn(raw[:, j, :], misc_b[j % 2][:, :], ACT.Copy).then_inc(qk_raw, 1)

            def norm_qk(s):
                act.wait_ge(qk_sum, (s + 1) * NJ)
                inverse_root(n_act, s * 2, ssq[:, :], nln[:, :], ny[:, :], eps_l2[:, :])

            def v_high(s, j):
                t, w = divmod(j, 2)
                act.wait_ge(v_ready, s * 2 * T + j + 1)
                fn(Vh[:, t, w * 512:(w + 1) * 512], misc_b[j % 2][:, :], ACT.Copy,
                   scale=1.0 / WS).then_inc(v_hi, 1)

            def copy_turned(s, n):
                act.wait_ge(t_ready, s * NT + n + 1)
                dst, src = turned(n)
                fn(dst, src, ACT.Copy).then_inc(t_odd, 1)

            def root_o(s):
                act.wait_ge(o_vec, s * KO + 4)
                inverse_root(o_act, s * KOA, omv[:, :, 1], oln[:, :], oy[:, :], eps_ln[:, :])

            def gate_exps(s):
                act.wait_ge(o_vec, s * KO + 17)
                for t in range(T):
                    fn(ge[:, t, :], gl[:, t, :], ACT.Exp, accum_out=gs[:, t:t + 1]).then_inc(o_act, 1)

            def exps(s, h):
                act.wait_ge(nb_done, s * H + h + 1)
                if h < 3:
                    from_one(act, p_lo, s * H)
                else:
                    act.wait_ge(p_lo, s * H + h - 2)
                for t in range(T):
                    keys = (t + 1) * P
                    fn(P32[:, h % 3, t * P:t * P + keys], score_b[h % 2][:, t * P:t * P + keys], ACT.Exp,
                       bias=nb[:, h % 2, t:t + 1], scale=rq10[:, t, h:h + 1],
                       accum_out=rs[:, h // GH, t, h % GH:h % GH + 1]).then_inc(ex_done, 1)

            def copy_pt(s, h):
                act.wait_ge(pt_ready, s * H + h + 1)
                from_one(act, pv_done, s * H + h - 1)
                fn(PT[:, h % 2, :, :, :].rearrange("p a b q -> p (a b q)"),
                   turn_b[h % 2][:, :].bitcast(F16)[:, 0:6 * P], ACT.Copy).then_inc(pt_odd, 1)

            def copy_ot(s, g):
                act.wait_ge(ot_ready, s * NG + g + 1)
                if g == 0:
                    from_one(act, wo_ready, s)
                fn(OT[:, 2 * g:2 * g + 2, :].rearrange("p m q -> p (m q)"), sum_b[g % 2][:, :],
                   ACT.Copy).then_inc(ot_done, 1)

            def decay(s, d):
                if d == 0:
                    act.wait_ge(c_vec, s * KC + 5)
                fn(aexp[:, d, :], dt[:, :], ACT.Exp, scale=negA[:, d:d + 1]).then_inc(a_done, 1)

            def step_tanh(s):
                act.wait_ge(dt_ready, s + 1)
                fn(th[:, :], misc_b[1][:, 0:SEQ], ACT.Tanh, bias=half_dtb[:, :], scale=0.5
                   ).then_inc(tanh_done, 1)

            def gelus(s, e):
                for q in (2 * e, 2 * e + 1):
                    act.wait_ge(w1_ready, s * NE * 2 + q + 1)
                    if q % 2 == 0 and e >= 2:
                        act.wait_ge(w2_ready, s * NE * T + T * (e - 1))
                    for m in range(2):
                        f = 2 * q + m
                        fn(hid[:, e % 2, f % FC, :], score_b[q % 2][:, m * SEQ:(m + 1) * SEQ],
                           ACT.Gelu_apprx_tanh, bias=b1c[:, f:f + 1], scale=1.0 / WS).then_inc(gelu_done, 1)

            def last_norm(s):
                act.wait_ge(e_vec, s * KE + 4)
                inverse_root(e_act, s * 2, emv[:, :, 1], eln[:, :], ey[:, :], eps_ln[:, :])

            def prologue():
                for dst, src in ((dtw, dt_w), (b1r, b1.rearrange("e (c p) -> (e c) p", p=P)),
                                 (al, a_log), (bs, b), (cs, c), (gws, gate_w), (b2s, b2)):
                    act.dma_start(dst[:, :], src).then_inc(d_small, 16)
                for n, src in enumerate((ln_g, ln_b, dt_b, conv_b)):
                    act.dma_start(cols[:, n:n + 1], src.unsqueeze(1)).then_inc(d_small, 16)
                act.dma_start(cols[:, 4:7], conv_w.rearrange("p a k -> p (a k)")).then_inc(d_small, 16)
                act.dma_start(grow[:, :], ln_g.partition_broadcast(P)).then_inc(d_small, 16)
                act.dma_start(brow[:, :], ln_b.partition_broadcast(P)).then_inc(d_small, 16)
                act.dma_start(gbrow[:, :], gate_b.partition_broadcast(P)).then_inc(d_small, 16)
                act.dma_start(crow[:, :], q_scale.rearrange("h a d -> (h a d)").partition_broadcast(P)
                              ).then_inc(d_small, 16)
                act.dma_start(krow, k_scale.rearrange("h a d -> (h a d)").partition_broadcast(P)
                              ).then_inc(d_small, 16)
                act.dma_start(wos[:, :, :], Wo.rearrange("(c p) n -> p c n", p=P)).then_inc(d_wo, 16)
                with_exp_and_ln()
                act.wait_ge(const_vec, 3)
                norm(0, 0)
                act.wait_ge(d_w, 48)
                fn(wh[:, :], W32, ACT.Copy, scale=WS).then_inc(w_high, 1)
                norm(0, 1)
                act.wait_ge(d_small, 16 * 17)
                fn(spt[:, 0, :], al[:, :], ACT.Abs).then_inc(setup_act, 1)
                act.wait_ge(setup_act, 1)
                fn(spt[:, 1, :], spt[:, 0, :], ACT.Exp, scale=-1.0).then_inc(setup_act, 1)
                act.wait_ge(setup_act, 2)
                fn(spt[:, 2, :], spt[:, 1, :], ACT.Ln, bias=1.0).then_inc(setup_act, 1)
                act.wait_ge(w_low, 1)
                for j in range(NJ):
                    copy_raw(0, j)
                norm_qk(0)
                act.wait_ge(d_w1, 16)
                fn(w1h[:, :], W132, ACT.Copy, scale=WS).then_inc(w1_high, 1)
                act.wait_ge(setup_vec, 4)
                for j in range(2 * T):
                    v_high(0, j)
                for n in range(1, NT, 2):
                    copy_turned(0, n)
                norm(1, 0)
                norm(1, 1)
                with_gelu_and_tanh()
                step_tanh(0)
                with_exp_and_ln()

            def heads(i, k):
                if 4 <= k < H + 4 and k % 2 == 1:
                    copy_pt(i, k - 4)
                if k in (11, 15, 19):
                    copy_ot(i, (k - 11) // GH)
                if k == 21:
                    copy_ot(i, NG - 1)

            def body(i, older, old, new, newer):
                for k in range(H + 1):
                    if older and k == 0:
                        last_norm(i - 2)
                    if new and 3 <= k < 3 + NJ:
                        copy_raw(i + 1, k - 3)
                    heads(i, k)
                    if new and k == 13:
                        norm_qk(i + 1)
                    if old and k == 12:
                        root_o(i - 1)
                    if newer and k == 4:
                        norm(i + 2, 0)
                    if newer and k == 8:
                        norm(i + 2, 1)
                    if k >= 1:
                        exps(i, k - 1)
                        decay(i, k - 1)
                if old:
                    gate_exps(i - 1)
                with_gelu_and_tanh()
                for m in range(NE + 2):
                    if new and m in (3, 5):
                        v_high(i + 1, m - 3)
                        v_high(i + 1, m - 2)
                    if new and 3 <= m < 8:
                        copy_turned(i + 1, 2 * m - 5)
                    for k in (H + 1 + 2 * m, H + 2 + 2 * m):
                        heads(i, k)
                    if old and m < NE:
                        gelus(i - 1, m)
                    if new and m == 7:
                        step_tanh(i + 1)
                with_exp_and_ln()

            def tail():
                last_norm(LAST - 1)
                root_o(LAST)
                gate_exps(LAST)
                with_gelu_and_tanh()
                for e in range(NE):
                    gelus(LAST, e)
                with_exp_and_ln()
                last_norm(LAST)

            bodies(act, prologue, body, tail)

        @block.gpsimd
        def _(pool):
            def square(s, j):
                pool.wait_ge(qk_raw, s * NJ + j + 1)
                from_one(pool, qk_sum, s * NJ + j - 1)
                nc.gpsimd.tensor_tensor(sq[:, j % 2, :], raw[:, j, :], raw[:, j, :], ALU.mult
                                        ).then_inc(qk_sq, 1)

            def q_low(s, n):
                t, w = divmod(n, 2)
                pool.wait_ge(q_hi, s * 2 * T + n + 1)
                pair = Qs[:, t, 4 * w:4 * w + 4, :, :]
                src = qc[:, n % 2, :].rearrange("p (a h d) -> p a h d", h=2, d=DH)
                nc.gpsimd.tensor_tensor(pair[:, :, 1:3, :], src, pair[:, :, 0:4:3, :], ALU.subtract
                                        ).then_inc(q_lo, 1)

            def k_unit(s, n):
                t, w = divmod(n, 2)
                if n == 0:
                    pool.wait_ge(n_vec, s * KN + 4)
                c0 = t * 2 * H + H + w * 8
                nc.gpsimd.tensor_tensor(
                    raw[:, 4 * t + 2 + w, :].rearrange("p (h d) -> p h d", d=DH),
                    raw[:, 4 * t + 2 + w, :].rearrange("p (h d) -> p h d", d=DH),
                    nr[:, c0:c0 + 8].unsqueeze(2).broadcast_to([P, 8, DH]), ALU.mult).then_inc(k_norm, 1)

            def k_low(s, n):
                t, w = divmod(n, 2)
                pool.wait_ge(k_hi, s * 2 * T + n + 1)
                nc.gpsimd.tensor_tensor(
                    Kl[:, t, w * 512:(w + 1) * 512].rearrange("p (h d) -> p h d", d=DH),
                    raw[:, 4 * t + 2 + w, :].rearrange("p (h d) -> p h d", d=DH),
                    Kh[:, t, w * 8:(w + 1) * 8, 0, :], ALU.subtract).then_inc(k_lo, 1)

            def p_low(s, h):
                pool.wait_ge(p_hi, s * H + h + 1)
                nc.gpsimd.tensor_tensor(Pl[:, h % 2, :], P32[:, h % 3, :], Ph[:, h % 2, :], ALU.subtract
                                        ).then_inc(p_lo, 1)

            def x_bias(s):
                pool.wait_ge(xres_loaded, 16 * (s + 1))
                from_one(pool, xy_done, s)
                nc.gpsimd.tensor_tensor(xb[:, :, :], xres[:, :, :],
                                        brow[:, :].unsqueeze(1).broadcast_to([P, T, D]), ALU.add
                                        ).then_inc(xb_done, 1)

            def prologue():
                nc.gpsimd.memset(ident[:, :], 0.0).then_inc(const_pool, 1)
                nc.gpsimd.memset(mask[:, :], 0.0).then_inc(const_pool, 1)
                pool.wait_ge(const_pool, 2)
                nc.gpsimd.affine_select(out=ident[:, :], in_=ident[:, :], compare_op=ALU.not_equal, fill=1.0,
                                        base=0, pattern=[[-1, P]], channel_multiplier=1
                                        ).then_inc(const_pool, 1)
                nc.gpsimd.affine_select(out=mask[:, :], in_=mask[:, :], compare_op=ALU.is_ge, fill=MASKED,
                                        base=0, pattern=[[-1, P]], channel_multiplier=1
                                        ).then_inc(const_pool, 1)
                pool.wait_ge(d_small, 16 * 17)
                pool.wait_ge(setup_vec, 2)
                for j in range(NJ):
                    square(0, j)
                    if j % 4 == 3:
                        q_low(0, 2 * (j // 4))
                        q_low(0, 2 * (j // 4) + 1)
                for n in range(2 * T):
                    k_unit(0, n)
                for n in range(2 * T):
                    k_low(0, n)

            def body(i, older, old, new, newer):
                for k in range(H + 2):
                    if old and k == 0:
                        x_bias(i - 1)
                    if new and 4 <= k < 4 + NJ:
                        square(i + 1, k - 4)
                    if new and k in (6, 7, 10, 11):
                        q_low(i + 1, (6, 7, 10, 11).index(k))
                    if new and k in (15, 16):
                        k_unit(i + 1, 2 * k - 30)
                        k_unit(i + 1, 2 * k - 29)
                    if 2 <= k:
                        p_low(i, k - 2)
                if new:
                    for n in range(2 * T):
                        k_low(i + 1, n)

            def tail():
                x_bias(LAST)

            bodies(pool, prologue, body, tail)

        @block.vector
        def _(dve):
            V = nc.vector

            def root_step(n, semaphore, done, root_ready, ve, y0, a, b_, dst, src, eps):
                if n == 0:
                    dve.wait_ge(semaphore, done)
                    V.tensor_scalar(ve, src, eps, None, ALU.add).then_inc(semaphore, 1)
                    dve.wait_ge(*root_ready)
                    dve.wait_ge(semaphore, done + 1)
                    V.scalar_tensor_tensor(a, y0, -0.5, ve, ALU.mult, ALU.mult).then_inc(semaphore, 1)
                elif n == 1:
                    dve.wait_ge(semaphore, done + 2)
                    V.tensor_tensor(b_, a, y0, ALU.mult).then_inc(semaphore, 1)
                else:
                    dve.wait_ge(semaphore, done + 3)
                    V.scalar_tensor_tensor(dst, b_, 1.5, y0, ALU.add, ALU.mult).then_inc(semaphore, 1)

            def stats(semaphore, src, st6):
                for t in range(T):
                    V.bn_stats(st6[:, t, :], src(t)).then_inc(semaphore, 1)

            def aggregate(semaphore, done, st6, mv):
                dve.wait_ge(semaphore, done)
                V.memset(pad[:, :], 0.0)
                for t in range(T):
                    V.bn_aggr(mv[:, t, :], st6[:, t, :]).then_inc(semaphore, 1)

            def normalise(semaphore, done, dst, src, mv, r):
                dve.wait_ge(semaphore, done)
                for t in range(T):
                    V.tensor_scalar(dst[:, t, :], src(t), mv[:, t, 0:1], r[:, t:t + 1],
                                    ALU.subtract, ALU.mult).then_inc(semaphore, 1)

            def g_step(s, n):
                at = s * KG
                if n < 12:
                    src = (lambda t: xin[:, t, :]) if n < 6 else (lambda t: xn[:, t, :])
                    at += 10 * (n // 6)
                if n in (0, 6):
                    if n == 0:
                        dve.wait_ge(x_loaded, 16 * (s + 1))
                    else:
                        dve.wait_ge(g_vec, at)
                    stats(g_vec, src, gst)
                elif n in (1, 7):
                    aggregate(g_vec, at + 2, gst, gmv)
                elif n in (2, 3, 4, 8, 9, 10):
                    root_step(n % 6 - 2, g_vec, at + 4, (g_act, s * KGA + 2 + 2 * (n // 6)), gve[:, :],
                              gy[:, :], gu[:, :], gw[:, :], gr[:, :], gmv[:, :, 1], LN_EPS)
                elif n in (5, 11):
                    normalise(g_vec, at + 8, (xn, z)[n // 6], src, gmv, gr)
                elif n == 12:
                    dve.wait_ge(g_tr, s + 1)
                    V.tensor_copy(xnT[:, 1:SEQ + 1], misc_b[0][:, 0:SEQ]).then_inc(g_vec, 1)
                    V.tensor_scalar(hT[:, :], misc_b[0][:, SEQ:2 * SEQ], lng, lnb, ALU.mult, ALU.add
                                    ).then_inc(g_vec, 1)
                elif n == 13:
                    dve.wait_ge(g_vec, at + 22)
                    V.tensor_copy(hTh[:, :], hT[:, :]).then_inc(g_vec, 1)
                else:
                    dve.wait_ge(g_vec, at + 23)
                    V.tensor_tensor(hTl[:, :], hT[:, :], hTh[:, :], ALU.subtract).then_inc(g_vec, 1)

            def qk_sums(s, j):
                dve.wait_ge(qk_sq, s * NJ + j + 1)
                V.tensor_reduce(ssq[:, j * 8:(j + 1) * 8], sq[:, j % 2, :].rearrange("p (h d) -> p h d", d=DH),
                                AX.X, ALU.add).then_inc(qk_sum, 1)

            def q_scaled(s, j):
                t, w = divmod(j, 4)
                n = 2 * t + w
                dve.wait_ge(qk_raw, s * NJ + j + 1)
                from_one(dve, q_lo, s * 2 * T + n - 1)
                V.tensor_tensor(qc[:, n % 2, :], raw[:, j, :], crow[:, w * 512:(w + 1) * 512], ALU.mult
                                ).then_inc(qc_done, 1)

            def q_high(s, j):
                t, w = divmod(j, 4)
                n = 2 * t + w
                dve.wait_ge(qc_done, s * 2 * T + n + 1)
                V.tensor_copy(Qs[:, t, 4 * w:4 * w + 4, 0:4:3, :],
                              qc[:, n % 2, :].rearrange("p (a h d) -> p a h d", h=2, d=DH)).then_inc(q_hi, 1)

            def norm_step(s, n):
                if n == 0:
                    dve.wait_ge(qk_sum, (s + 1) * NJ)
                from_zero = s * KN
                if n == 0:
                    V.tensor_scalar(nve[:, :], ssq[:, :], L2_EPS * WS * WS, None, ALU.add).then_inc(n_vec, 1)
                    dve.wait_ge(n_act, s * 2 + 2)
                    dve.wait_ge(n_vec, from_zero + 1)
                    V.scalar_tensor_tensor(nu[:, :], ny[:, :], -0.5, nve[:, :], ALU.mult, ALU.mult
                                           ).then_inc(n_vec, 1)
                elif n == 1:
                    dve.wait_ge(n_vec, from_zero + 2)
                    V.tensor_tensor(nw[:, :], nu[:, :], ny[:, :], ALU.mult).then_inc(n_vec, 1)
                else:
                    dve.wait_ge(n_vec, from_zero + 3)
                    V.scalar_tensor_tensor(nr[:, :], nw[:, :], 1.5, ny[:, :], ALU.add, ALU.mult
                                           ).then_inc(n_vec, 1)

            def scale_q(s):
                dve.wait_ge(n_vec, s * KN + 4)
                V.tensor_scalar(rq10[:, :, :], nr[:, :].rearrange("p (t w h) -> p t w h", t=T, w=2)[:, :, 0, :],
                                QK_SCALE * WS, None, ALU.mult).then_inc(n_vec, 1)

            def k_high(s, t):
                for n in (2 * t, 2 * t + 1):
                    t, w = divmod(n, 2)
                    dve.wait_ge(k_norm, s * 2 * T + n + 1)
                    V.tensor_copy(Kh[:, t, w * 8:(w + 1) * 8, :, :],
                                  raw[:, 4 * t + 2 + w, :].rearrange("p (h d) -> p h d", d=DH).unsqueeze(2)
                                  .broadcast_to([P, 8, 2, DH])).then_inc(k_hi, 1)

            def v_low(s, j):
                t, w = divmod(j, 2)
                dve.wait_ge(v_hi, s * 2 * T + j + 1)
                V.scalar_tensor_tensor(Vl[:, t, w * 512:(w + 1) * 512], misc_b[j % 2][:, :], 1.0 / WS,
                                       Vh[:, t, w * 512:(w + 1) * 512], ALU.mult, ALU.subtract
                                       ).then_inc(v_lo, 1)

            def copy_turned(s, n):
                dve.wait_ge(t_ready, s * NT + n + 1)
                dst, src = turned(n)
                V.tensor_copy(dst, src).then_inc(t_even, 1)

            def maxima(s, h):
                dve.wait_ge(sc_ready, s * H + h + 1)
                for t in range(T):
                    V.tensor_reduce(mx[:, h % 2, t:t + 1], score_b[h % 2][:, t * P:t * P + (t + 1) * P], AX.X,
                                    ALU.max, negate=True).then_inc(mx_done, 1)

            def biases(s, h):
                dve.wait_ge(mx_done, s * H * T + (h + 1) * T)
                if h == 0:
                    dve.wait_ge(n_vec, (s + 1) * KN)
                V.tensor_tensor(nb[:, h % 2, :], mx[:, h % 2, :], rq10[:, :, h], ALU.mult).then_inc(nb_done, 1)

            def p_high(s, h):
                dve.wait_ge(ex_done, s * 2 * H + 2 * h + 2)
                from_one(dve, pt_ready, s * H + h - 1)
                V.tensor_copy(Ph[:, h % 2, :], P32[:, h % 3, :]).then_inc(p_hi, 1)

            def copy_pt(s, h):
                dve.wait_ge(pt_ready, s * H + h + 1)
                from_one(dve, pv_done, s * H + h - 1)
                V.tensor_copy(PT[:, h % 2, :, :, :].rearrange("p a b q -> p (a b q)"),
                              turn_b[h % 2][:, :].bitcast(F16)[:, 0:6 * P]).then_inc(pt_even, 1)

            def inverse_sums(s, g):
                dve.wait_ge(ex_done, s * 2 * H + 2 * GH * (g + 1))
                V.reciprocal(rr[:, g % 2, :], rs[:, g, :, :].rearrange("p t h -> p (t h)")).then_inc(rr_done, 1)

            def divide(s, g):
                dve.wait_ge(rr_done, s * NG + g + 1)
                dve.wait_ge(pv_done, s * H + GH * (g + 1))
                V.tensor_tensor(On[:, g % 2, :, :].rearrange("p t (h d) -> p (t h) d", d=DH),
                                sum_b[g % 2][:, :].rearrange("p (a d) -> p a d", d=DH),
                                rr[:, g % 2, :].unsqueeze(2).broadcast_to([P, T * GH, DH]), ALU.mult
                                ).then_inc(on_done, 1)

            def o_step(s, n):
                at = s * KO
                o0, o1 = misc_b
                src = lambda t: o0[:, t * P:(t + 1) * P]
                if n == 0:
                    dve.wait_ge(wo_ready, s + 1)
                    stats(o_vec, src, ost)
                elif n == 1:
                    aggregate(o_vec, at + 2, ost, omv)
                elif n <= 4:
                    root_step(n - 2, o_vec, at + 4, (o_act, s * KOA + 2), ove[:, :], oy[:, :], ou[:, :],
                              ow[:, :], orr[:, :], omv[:, :, 1], LN_EPS)
                elif n == 5:
                    normalise(o_vec, at + 8, z2, src, omv, orr)
                elif n == 6:
                    dve.wait_ge(o_tr, s + 1)
                    V.tensor_scalar(h2T[:, :], o1[:, 0:SEQ], lng, lnb, ALU.mult, ALU.add
                                    ).then_inc(o_vec, 1)
                elif n == 7:
                    dve.wait_ge(o_vec, at + 11)
                    V.tensor_copy(h2h[:, :], h2T[:, :]).then_inc(o_vec, 1)
                elif n == 8:
                    dve.wait_ge(o_vec, at + 12)
                    V.tensor_tensor(h2l[:, :], h2T[:, :], h2h[:, :], ALU.subtract).then_inc(o_vec, 1)
                elif n == 9:
                    dve.wait_ge(o_gate, s + 1)
                    V.tensor_tensor(gl[:, :, :], o0[:, 0:T * NE].rearrange("p (t e) -> p t e", t=T),
                                    gbrow[:, :].unsqueeze(1).broadcast_to([P, T, NE]), ALU.add
                                    ).then_inc(o_vec, 1)
                elif n == 10:
                    dve.wait_ge(o_vec, at + 14)
                    V.tensor_reduce(gm[:, :], gl[:, :, :], AX.X, ALU.max).then_inc(o_vec, 1)
                elif n == 11:
                    dve.wait_ge(o_vec, at + 15)
                    for t in range(T):
                        V.tensor_scalar(gl[:, t, :], gl[:, t, :], gm[:, t:t + 1], None, ALU.subtract
                                        ).then_inc(o_vec, 1)
                elif n == 12:
                    dve.wait_ge(o_act, (s + 1) * KOA)
                    V.reciprocal(grs[:, :], gs[:, :]).then_inc(o_vec, 1)
                elif n == 13:
                    dve.wait_ge(o_vec, at + 18)
                    for t in range(T):
                        V.tensor_scalar(gate[:, t, 0:NE], ge[:, t, :], grs[:, t:t + 1], None, ALU.mult
                                        ).then_inc(o_vec, 1)
                elif n == 14:
                    dve.wait_ge(o_gT, s + 1)
                    V.tensor_copy(gateT[:, :], o1[:, 0:SEQ]).then_inc(o_vec, 1)
                else:
                    dve.wait_ge(o_b2, s + 1)
                    V.tensor_copy(acc[:, :, :].rearrange("p t d -> p (t d)"), o0[:, 0:SEQ]
                                  ).then_inc(o_vec, 1)

            def add_expert(s, e, t):
                if t == 0:
                    dve.wait_ge(w2_ready, s * NE * T + (e + 1) * T)
                if e > 0:
                    dve.wait_ge(acc_done, s * NE * T + (e - 1) * T + t + 1)
                elif t == 0:
                    dve.wait_ge(o_vec, (s + 1) * KO)
                V.scalar_tensor_tensor(acc[:, t, :], sum_b[e % 2][:, t * P:(t + 1) * P],
                                       gate[:, t, e:e + 1], acc[:, t, :], ALU.mult, ALU.add
                                       ).then_inc(acc_done, 1)

            def convolve(s, n):
                if n == 0:
                    V.tensor_scalar(cv[:, 0, :], xnT[:, 1:SEQ + 1], cols[:, 5:6], cb, ALU.mult, ALU.add
                                    ).then_inc(c_vec, 1)
                else:
                    dve.wait_ge(c_vec, s * KC + n)
                    V.scalar_tensor_tensor((cv[:, 1, :], xf[:, :])[n - 1], xnT[:, 2 * n - 2:2 * n - 2 + SEQ],
                                           cols[:, 2 * n + 2:2 * n + 3], cv[:, n - 1, :], ALU.mult, ALU.add
                                           ).then_inc(c_vec, 1)

            def step_inputs(s, n):
                if n == 0:
                    dve.wait_ge(tanh_done, s + 1)
                    half = 0.5 * (DT_MAX - DT_MIN)
                    V.tensor_scalar(dt[:, :], th[:, :], half, half + DT_MIN, ALU.mult, ALU.add
                                    ).then_inc(c_vec, 1)
                else:
                    dve.wait_ge(c_vec, s * KC + 4)
                    V.tensor_tensor(u[:, :], dt[:, :], xf[:, :], ALU.mult).then_inc(c_vec, 1)

            def scan(s, d):
                dve.wait_ge(a_done, s * DS + d + 1)
                if d == 0:
                    dve.wait_ge(c_vec, (s + 1) * KC)
                from_one(dve, y_done, s * DS + d - 1)
                V.tensor_tensor_scan(st[:, d % 2, :], aexp[:, d, :], u[:, :], 0.0, ALU.mult, ALU.add
                                     ).then_inc(scan_done, 1)

            def add_state(s, d):
                dve.wait_ge(scan_done, s * DS + d + 1)
                if d == 0:
                    V.tensor_scalar(y[:, :], st[:, 0, :], bc[:, 0:1], None, ALU.mult).then_inc(y_done, 1)
                else:
                    dve.wait_ge(y_done, s * DS + d)
                    V.scalar_tensor_tensor(y[:, :], st[:, d % 2, :], bc[:, d:d + 1], y[:, :],
                                           ALU.mult, ALU.add).then_inc(y_done, 1)

            def e_step(s, n):
                at = s * KE
                if n == 0:
                    dve.wait_ge(acc_done, (s + 1) * NE * T)
                    stats(e_vec, lambda t: acc[:, t, :], est)
                elif n == 1:
                    aggregate(e_vec, at + 2, est, emv)
                elif n <= 4:
                    root_step(n - 2, e_vec, at + 4, (e_act, s * 2 + 2), eve[:, :], ey[:, :], eu[:, :],
                              ew[:, :], er[:, :], emv[:, :, 1], LN_EPS)
                elif n == 5:
                    normalise(e_vec, at + 8, e1, lambda t: acc[:, t, :], emv, er)
                elif n == 6:
                    dve.wait_ge(e_vec, at + 10)
                    V.tensor_tensor(e2[:, :, :], e1[:, :, :],
                                    grow[:, :].unsqueeze(1).broadcast_to([P, T, D]), ALU.mult
                                    ).then_inc(e_vec, 1)
                else:
                    dve.wait_ge(e_vec, at + 11)
                    dve.wait_ge(fin_free, 16 * (s + 1))
                    dve.wait_ge(xy_done, s + 1)
                    V.tensor_tensor(fin[:, :, :], e2[:, :, :], xy[:, :, :], ALU.add).then_inc(e_vec, 1)

            def add_y(s):
                dve.wait_ge(xb_done, s + 1)
                dve.wait_ge(y_tr, s + 1)
                from_one(dve, e_vec, s * KE)
                V.tensor_tensor(xy[:, :, :].rearrange("p t d -> p (t d)"), misc_b[1][:, 0:SEQ],
                                xb[:, :, :].rearrange("p t d -> p (t d)"), ALU.add).then_inc(xy_done, 1)

            def prologue():
                V.memset(pad[:, :], 0.0).then_inc(fin_free, 16)
                V.memset(eps_ln[:, :], LN_EPS)
                V.memset(eps_l2[:, :], L2_EPS * WS * WS)
                V.memset(xnT[:, :], 0.0)
                V.memset(gate[:, :, :].rearrange("p t e -> p (t e)"), 0.0)
                dve.wait_ge(const_pool, 4)
                V.tensor_copy(ident16[:, :], ident[:, :]).then_inc(const_vec, 1)
                V.tensor_copy(identb[:, :], ident[:, :]).then_inc(const_vec, 1)
                V.tensor_copy(maskb[:, :], mask[:, :]).then_inc(const_vec, 1)
                for n in range(12):
                    g_step(0, n)
                dve.wait_ge(w_high, 1)
                V.scalar_tensor_tensor(wl[:, :], W32, WS, wh[:, :], ALU.mult, ALU.subtract).then_inc(w_low, 1)
                dve.wait_ge(setup_tr, 1)
                dve.wait_ge(d_small, 16 * 17)
                V.tensor_copy(dtwT[:, :], misc_b[1][:, 0:D])
                V.tensor_copy(b1c[:, :], misc_b[1][:, D:D + NE * FC]).then_inc(setup_vec, 1)
                V.tensor_scalar(half_dtb[:, :], dtb, 0.5, None, ALU.mult)
                V.tensor_tensor(bc[:, :], bs[:, :], cs[:, :], ALU.mult)
                V.scalar_tensor_tensor(crow[:, :], crow[:, :], 1.0 / WS, krow, ALU.mult, ALU.mult
                                       ).then_inc(setup_vec, 1)
                dve.wait_ge(setup_vec, 2)
                for n in range(12, 15):
                    g_step(0, n)
                for j in range(NJ):
                    qk_sums(0, j)
                    if j % 4 < 2:
                        q_scaled(0, j)
                        q_high(0, j)
                dve.wait_ge(setup_act, 3)
                V.scalar_tensor_tensor(spt[:, 3, :], al[:, :], 0.0, spt[:, 2, :], ALU.max, ALU.add
                                       ).then_inc(setup_vec, 1)
                dve.wait_ge(setup_vec, 3)
                V.tensor_scalar(negA[:, :], spt[:, 3, :], -1.0, None, ALU.mult).then_inc(setup_vec, 1)
                for n in range(3):
                    norm_step(0, n)
                scale_q(0)
                for j in range(2 * T):
                    v_low(0, j)
                k_high(0, 0)
                k_high(0, 1)
                for n in range(0, NT, 2):
                    copy_turned(0, n)
                for n in range(3):
                    convolve(0, n)
                for n in range(15):
                    g_step(1, n)
                dve.wait_ge(w1_high, 1)
                V.scalar_tensor_tensor(w1l[:, :], W132, WS, w1h[:, :], ALU.mult, ALU.subtract
                                       ).then_inc(w1_low, 1)
                step_inputs(0, 0)
                step_inputs(0, 1)

            E_AT = {(1, 0): 2, (1, 1): 3, (1, 2): 4, (2, 0): 5, (2, 1): 6, (2, 2): 7}
            G_AT = {(3, 0): 0, (3, 2): 1, (5, 0): 2, (5, 1): 3, (5, 2): 4, (6, 0): 5, (7, 0): 6, (7, 2): 7,
                    (9, 0): 8, (9, 1): 9, (9, 2): 10, (10, 0): 11}
            O_AT = {(11, 0): 0, (11, 2): 1, (12, 0): 2, (12, 1): 3, (12, 2): 4, (13, 0): 5, (14, 0): 6,
                    (14, 1): 7, (14, 2): 8, (16, 0): 9, (16, 1): 10, (16, 2): 11}
            N_AT = {(13, 1): 0, (13, 2): 1, (14, 0): 2}

            def body(i, older, old, new, newer):
                def between(k, place):
                    if older and (k, place) in E_AT:
                        e_step(i - 2, E_AT[k, place])
                    if newer and (k, place) in G_AT:
                        g_step(i + 2, G_AT[k, place])
                    if old and (k, place) in O_AT:
                        o_step(i - 1, O_AT[k, place])
                    if new and (k, place) in N_AT:
                        norm_step(i + 1, N_AT[k, place])

                for k in range(H + 1):
                    j = k - 5
                    if k >= 1:
                        maxima(i, k - 1)
                    if k >= 2:
                        p_high(i, k - 2)
                    if k >= 1:
                        biases(i, k - 1)
                    between(k, 0)
                    if k >= 9 and k % GH == 1:
                        inverse_sums(i, (k - 9) // GH)
                    if k >= 4 and k % 2 == 0:
                        copy_pt(i, k - 4)
                    if new and 0 <= j < NJ:
                        qk_sums(i + 1, j)
                    between(k, 1)
                    if k >= 9 and k % GH == 1:
                        divide(i, (k - 9) // GH)
                    if new and 0 <= j < NJ and j % 4 < 2:
                        q_scaled(i + 1, j)
                    between(k, 2)
                    if new and 0 <= j < NJ and j % 4 < 2:
                        q_high(i + 1, j)
                    if old and k == 2:
                        add_y(i - 1)
                for m in range(NE + 2):
                    if m == 0:
                        p_high(i, H - 1)
                        inverse_sums(i, 2)
                        if old:
                            o_step(i - 1, 12)
                        divide(i, 2)
                        if old:
                            o_step(i - 1, 13)
                        copy_pt(i, H - 2)
                        inverse_sums(i, 3)
                    if new and m in (1, 2):
                        k_high(i + 1, m - 1)
                    if new and m == 1:
                        scale_q(i + 1)
                    if new and 3 <= m < 8:
                        copy_turned(i + 1, 2 * m - 6)
                    if old and m >= 2:
                        add_expert(i - 1, m - 2, 0)
                    if m < NE:
                        scan(i, 2 * m)
                    if old and m >= 2:
                        add_expert(i - 1, m - 2, 1)
                    if m < NE:
                        scan(i, 2 * m + 1)
                        add_state(i, 2 * m)
                    if old and m == 0:
                        o_step(i - 1, 14)
                    if new and m in (3, 5):
                        v_low(i + 1, m - 3)
                        v_low(i + 1, m - 2)
                    if new and m in (2, 3, 4):
                        convolve(i + 1, m - 2)
                    if newer and m == 7:
                        g_step(i + 2, 12)
                    if m < NE:
                        add_state(i, 2 * m + 1)
                    if newer and m == 7:
                        g_step(i + 2, 13)
                        g_step(i + 2, 14)
                    if old and m == 1:
                        o_step(i - 1, 15)
                    if m == 1:
                        divide(i, 3)
                    if new and m >= NE:
                        step_inputs(i + 1, m - NE)
                if old:
                    e_step(i - 1, 0)
                    e_step(i - 1, 1)

            def tail():
                for n in range(2, 8):
                    e_step(LAST - 1, n)
                add_y(LAST)
                for n in range(16):
                    o_step(LAST, n)
                for e in range(NE):
                    add_expert(LAST, e, 0)
                    add_expert(LAST, e, 1)
                for n in range(8):
                    e_step(LAST, n)

            bodies(dve, prologue, body, tail)


_INS = ['x', 'a_log', 'b', 'c', 'dt_w', 'dt_b', 'conv_w', 'conv_b']
_FFN = ['ln_g', 'ln_b', 'Wq', 'Wk', 'Wv', 'q_scale', 'k_scale', 'Wo', 'gate_w', 'gate_b', 'w1', 'b1', 'w2', 'b2']


def kernel(**inputs):
    import concourse.bacc as bacc
    from concourse.bass_utils import run_bass_kernel_spmd

    nc = bacc.Bacc("TRN2", target_bir_lowering=False, num_devices=1)
    arrays, args = {}, []
    for name in [f"L0_attn_{n}" for n in _INS] + [f"L0_ffn_{n}" for n in _FFN]:
        a = np.ascontiguousarray(inputs[name])
        arrays[f"in_{name}"] = a
        args.append(nc.dram_tensor(f"in_{name}", a.shape, mybir.dt.from_np(a.dtype), kind="ExternalInput").ap())
    shape = inputs["L0_attn_x"].shape
    args.append(nc.dram_tensor("out_dram", shape, F32, kind="ExternalOutput").ap())
    build(nc, *args)
    r = run_bass_kernel_spmd(nc, [arrays], core_ids=[0])
    return r.results[0]["out_dram"]
```

```python
from contextlib import ExitStack

import numpy as np
import concourse.bass as bass
from concourse import mybir
from concourse.alu_op_type import AluOpType as ALU

F32 = mybir.dt.float32
F16 = mybir.dt.float16
BF16 = mybir.dt.bfloat16
ACT = mybir.ActivationFunctionType
AX = mybir.AxisListType

NSEQ, SEQ, D = 16, 256, 128
P = 128
T = SEQ // P
H, DH = 16, 64
HD = H * DH
NE, FF = 8, 512
FC = FF // P
DS = 16
PT_ACT = (2, 5, 7, 10, 12)
GH = 4
NG = H // GH
PC = SEQ + P
NJ = 4 * T
NT = 5 * T
WS = 64.0
LN_EPS, L2_EPS = 1e-5, 1e-12
QK_SCALE = 10.0
DT_MIN, DT_MAX = 0.001, 0.1
MASKED = -1e9
LAST = NSEQ - 1

KG, KGA = 24, 4
KN = 4
KO, KOA = 22, 4
KE = 12
KC = 5


def build(nc, x, a_log, b, c, dt_w, dt_b, conv_w, conv_b, ln_g, ln_b, Wq, Wk, Wv, q_scale, k_scale,
          Wo, gate_w, gate_b, w1, b1, w2, b2, out):
    ctx = ExitStack()
    with ctx:
        def sb(name, shape, dt=F32):
            return ctx.enter_context(nc.sbuf_tensor(name, shape, dt))

        def sem(name):
            return ctx.enter_context(nc.semaphore(name))

        ident = sb("ident", [P, P])
        ident16 = sb("ident16", [P, P], F16)
        identb = sb("identb", [P, P], BF16)
        mask = sb("mask", [P, P])
        maskb = sb("maskb", [P, P], BF16)
        wh = sb("wh", [P, 3 * HD], F16)
        wl = sb("wl", [P, 3 * HD], F16)
        w1h = sb("w1h", [P, NE * FF], F16)
        w1l = sb("w1l", [P, NE * FF], F16)
        w2s = sb("w2s", [P, NE * FC, D])
        wos = sb("wos", [P, HD // P, D])
        crow = sb("crow", [P, HD])
        dtw = sb("dtw", [P, D])
        dtwT = sb("dtwT", [P, D])
        b1r = sb("b1r", [NE * FC, P])
        b1c = sb("b1c", [P, NE * FC])
        cols = sb("cols", [P, 8])
        lng, lnb, dtb, cb = (cols[:, n:n + 1] for n in range(4))
        half_dtb = sb("half_dtb", [P, 1])
        grow = sb("grow", [P, D])
        brow = sb("brow", [P, D])
        gbrow = sb("gbrow", [P, NE])
        gws = sb("gws", [P, NE])
        b2s = sb("b2s", [NE, D])
        al = sb("al", [P, DS])
        bs = sb("bs", [P, DS])
        cs = sb("cs", [P, DS])
        bc = sb("bc", [P, DS])
        spt = sb("spt", [P, 4, DS])
        negA = sb("negA", [P, DS])
        eps_ln = sb("eps_ln", [P, 1])
        eps_l2 = sb("eps_l2", [P, 1])
        pad = sb("pad", [P, 1])
        xin = sb("xin", [P, T, D])
        xn = sb("xn", [P, T, D])
        z = sb("z", [P, T, D])
        gst = sb("gst", [P, T, 6])
        gmv = sb("gmv", [P, T, 2])
        gve = sb("gve", [P, T])
        gln = sb("gln", [P, T])
        gy = sb("gy", [P, T])
        gu = sb("gu", [P, T])
        gw = sb("gw", [P, T])
        gr = sb("gr", [P, T])
        xnT = sb("xnT", [P, SEQ + 2])
        hT = sb("hT", [P, SEQ])
        hTh = sb("hTh", [P, SEQ], F16)
        hTl = sb("hTl", [P, SEQ], F16)
        raw = sb("raw", [P, NJ, 512])
        sq = sb("sq", [P, 2, 512])
        ssq = sb("ssq", [P, NJ * 8])
        nve = sb("nve", [P, NJ * 8])
        nln = sb("nln", [P, NJ * 8])
        ny = sb("ny", [P, NJ * 8])
        nu = sb("nu", [P, NJ * 8])
        nw = sb("nw", [P, NJ * 8])
        nr = sb("nr", [P, NJ * 8])
        Qs = sb("Qs", [P, T, H // 2, 4, DH], F16)
        Kh = sb("Kh", [P, T, H, 2, DH], F16)
        Kl = sb("Kl", [P, T, HD], F16)
        QT = sb("QT", [P, H, SEQ], F16)
        KT = sb("KT", [P, H, SEQ], F16)
        KL = sb("KL", [P, H // 2, SEQ], F16)
        Vh = sb("Vh", [P, T, HD], F16)
        Vl = sb("Vl", [P, T, HD], F16)
        mx = sb("mx", [P, 2, T])
        P32 = sb("P32", [P, 3, PC])
        Ph = sb("Ph", [P, 2, PC], F16)
        Pl = sb("Pl", [P, 2, PC], F16)
        PT = sb("PT", [P, 2, 2, 3, P], F16)
        rs = sb("rs", [P, NG, T, GH])
        rr = sb("rr", [P, 2, T * GH])
        On = sb("On", [P, 2, T, GH * DH])
        OT = sb("OT", [P, HD // P, SEQ])
        ost = sb("ost", [P, T, 6])
        omv = sb("omv", [P, T, 2])
        ove = sb("ove", [P, T])
        oln = sb("oln", [P, T])
        oy = sb("oy", [P, T])
        ou = sb("ou", [P, T])
        ow = sb("ow", [P, T])
        orr = sb("orr", [P, T])
        z2 = sb("z2", [P, T, D])
        h2T = sb("h2T", [P, SEQ])
        h2h = sb("h2h", [P, SEQ], F16)
        h2l = sb("h2l", [P, SEQ], F16)
        gl = sb("gl", [P, T, NE])
        gm = sb("gm", [P, T])
        ge = sb("ge", [P, T, NE])
        gs = sb("gs", [P, T])
        grs = sb("grs", [P, T])
        gate = sb("gate", [P, T, P])
        gateT = sb("gateT", [P, SEQ])
        hid = sb("hid", [P, 2, FC, SEQ])
        acc = sb("acc", [P, T, D])
        aexp = sb("aexp", [P, DS, SEQ])
        xf = sb("xf", [P, SEQ])
        cv = sb("cv", [P, 2, SEQ])
        th = sb("th", [P, SEQ])
        dt = sb("dt", [P, SEQ])
        u = sb("u", [P, SEQ])
        st = sb("st", [P, 2, SEQ])
        y = sb("y", [P, SEQ])
        est = sb("est", [P, T, 6])
        emv = sb("emv", [P, T, 2])
        eve = sb("eve", [P, T])
        eln = sb("eln", [P, T])
        ey = sb("ey", [P, T])
        eu = sb("eu", [P, T])
        ew = sb("ew", [P, T])
        er = sb("er", [P, T])
        e1 = sb("e1", [P, T, D])
        e2 = sb("e2", [P, T, D])
        xy = sb("xy", [P, T, D])
        fin = sb("fin", [P, T, D])
        xres = sb("xres", [P, T, D])
        xb = sb("xb", [P, T, D])
        krow = sq[:, :, :].rearrange("p a n -> p (a n)")
        W1COLS = NE // 2 * FF
        W32 = raw[:, 0:6, :].rearrange("p a n -> p (a n)")
        W132 = hid[:, :, :, :].rearrange("p r c n -> p (r c n)")

        bank = [ctx.enter_context(nc.psum_tensor(f"bank{n}", [P, 512], F32)) for n in range(8)]
        score_b = bank[0:2]
        turn_b = bank[2:4]
        sum_b = bank[4:6]
        misc_b = bank[6:8]

        names = """d_small d_cols d_w d_w1 d_w2 d_wo x_loaded xres_loaded fin_free
            const_pool const_vec w_high w_low w1_high w1_low setup_tr setup_vec setup_act
            g_vec g_act g_tr
            qk_ready qk_raw qk_sq qk_sum qc_done q_norm q_hi q_lo n_vec n_act k_norm k_hi k_lo
            v_ready v_hi v_lo t_ready t_done
            sc_ready mx_done ex_done p_hi p_lo pt_ready pt_dve pt_act pv_done rr_done on_done
            ot_ready ot_done
            wo_ready wo_copied o_vec o_act o_tr o_gate o_gT o_b2
            w1_ready gelu_done w2_ready acc_done
            c_vec dt_ready tanh_done a_done scan_done y_done
            y_tr e_vec e_act xb_done xy_done""".split()
        S = {n: sem(n) for n in names}
        (d_small, d_cols, d_w, d_w1, d_w2, d_wo, x_loaded, xres_loaded, fin_free,
         const_pool, const_vec, w_high, w_low, w1_high, w1_low, setup_tr, setup_vec, setup_act,
         g_vec, g_act, g_tr,
         qk_ready, qk_raw, qk_sq, qk_sum, qc_done, q_norm, q_hi, q_lo, n_vec, n_act, k_norm, k_hi, k_lo,
         v_ready, v_hi, v_lo, t_ready, t_done,
         sc_ready, mx_done, ex_done, p_hi, p_lo, pt_ready, pt_dve, pt_act, pv_done, rr_done, on_done,
         ot_ready, ot_done,
         wo_ready, wo_copied, o_vec, o_act, o_tr, o_gate, o_gT, o_b2,
         w1_ready, gelu_done, w2_ready, acc_done,
         c_vec, dt_ready, tanh_done, a_done, scan_done, y_done,
         y_tr, e_vec, e_act, xb_done, xy_done) = (S[n] for n in names)

        def tiles(ap):
            return ap.rearrange("(t p) d -> p t d", p=P)

        def turned(n):
            src = turn_b[n % 2][:, :].bitcast(F16).rearrange("p (m q) -> p m q", q=P)
            if n < 8:
                t, h = (n % 4) // 2, (n % 2) * 8
                return (KT, QT)[n // 4][:, h:h + 8, t * P:(t + 1) * P], src
            return KL[:, :, (n - 8) * P:(n - 7) * P], src

        def bodies(eng, prologue, body, tail):
            prologue()
            body(0, older=False, old=False, new=True, newer=True)
            body(1, older=False, old=True, new=True, newer=True)
            with eng.Fori(2, NSEQ - 2) as i:
                body(i, older=True, old=True, new=True, newer=True)
            body(NSEQ - 2, older=True, old=True, new=True, newer=False)
            body(LAST, older=True, old=True, new=False, newer=False)
            tail()

        def from_one(eng, semaphore, value):
            if not isinstance(value, int) or value > 0:
                eng.wait_ge(semaphore, value)

        def pt_copied(s, h):
            on_act = sum(n in PT_ACT for n in range(h + 1))
            if h in PT_ACT:
                return pt_act, s * len(PT_ACT) + on_act
            return pt_dve, s * (H - len(PT_ACT)) + h + 1 - on_act

        def square_on(eng, ops, s, j):
            eng.wait_ge(qk_raw, s * NJ + j + 1)
            from_one(eng, qk_sum, s * NJ + j - 1)
            ops.tensor_tensor(sq[:, j % 2, :], raw[:, j, :], raw[:, j, :], ALU.mult).then_inc(qk_sq, 1)

        def over_norm_on(eng, ops, s, n, part, done):
            t, w = divmod(n, 2)
            eng.wait_ge(n_vec, (s + 1) * KN)
            c0 = (2 * t + part) * H + w * 8
            group = raw[:, 4 * t + 2 * part + w, :].rearrange("p (h d) -> p h d", d=DH)
            ops.tensor_tensor(group, group, nr[:, c0:c0 + 8].unsqueeze(2).broadcast_to([P, 8, DH]), ALU.mult
                              ).then_inc(done, 1)

        def k_low_on(eng, ops, s, n):
            t, w = divmod(n, 2)
            eng.wait_ge(k_hi, s * 2 * T + n + 1)
            ops.tensor_tensor(Kl[:, t, w * 512:(w + 1) * 512].rearrange("p (h d) -> p h d", d=DH),
                              raw[:, 4 * t + 2 + w, :].rearrange("p (h d) -> p h d", d=DH),
                              Kh[:, t, w * 8:(w + 1) * 8, 0, :], ALU.subtract).then_inc(k_lo, 1)

        block = ctx.enter_context(nc.Block())

        @block.sync
        def _(sp):
            def load_x(s):
                if not isinstance(s, int) or s > 0:
                    sp.wait_ge(g_vec, (s - 1) * KG + 10)
                sp.dma_start(xin[:, :, :], tiles(x[s])).then_inc(x_loaded, 16)

            def load_xres(s):
                if not isinstance(s, int) or s > 0:
                    sp.wait_ge(xb_done, s)
                sp.dma_start(xres[:, :, :], tiles(x[s])).then_inc(xres_loaded, 16)

            def store_out(s):
                sp.wait_ge(e_vec, (s + 1) * KE)
                sp.dma_start(tiles(out[s]), fin[:, :, :]).then_inc(fin_free, 16)

            def load_w1(half):
                if half == 1:
                    sp.wait_ge(w1_low, 1)
                e0 = half * NE // 2
                sp.dma_start(W132.rearrange("p (e f) -> p e f", e=NE // 2),
                             w1[e0:e0 + NE // 2].rearrange("e p f -> p e f")).then_inc(d_w1, 16)

            def prologue():
                load_x(0)
                for n, w in enumerate((Wq, Wk, Wv)):
                    sp.dma_start(W32[:, n * HD:(n + 1) * HD], w).then_inc(d_w, 16)
                load_x(1)
                for dst, src in ((al, a_log), (bs, b), (cs, c), (gws, gate_w), (b2s, b2)):
                    sp.dma_start(dst[:, :], src).then_inc(d_small, 16)
                sp.dma_start(grow[:, :], ln_g.partition_broadcast(P)).then_inc(d_small, 16)
                sp.dma_start(brow[:, :], ln_b.partition_broadcast(P)).then_inc(d_small, 16)
                sp.dma_start(gbrow[:, :], gate_b.partition_broadcast(P)).then_inc(d_small, 16)
                sp.dma_start(crow[:, :], q_scale.rearrange("h a d -> (h a d)").partition_broadcast(P)
                              ).then_inc(d_small, 16)
                sp.dma_start(krow, k_scale.rearrange("h a d -> (h a d)").partition_broadcast(P)
                              ).then_inc(d_small, 16)
                sp.dma_start(w2s[:, :, :].rearrange("p (e c) n -> p e c n", e=NE),
                             w2.rearrange("e (c p) n -> p e c n", p=P)).then_inc(d_w2, 16)
                sp.dma_start(wos[:, :, :], Wo.rearrange("(c p) n -> p c n", p=P)).then_inc(d_wo, 16)
                load_xres(0)
                load_w1(0)

            def body(i, older, old, new, newer):
                if newer:
                    load_x(i + 2)
                if not old:
                    load_w1(1)
                if old:
                    load_xres(i)
                if older:
                    store_out(i - 2)

            def tail():
                store_out(LAST - 1)
                store_out(LAST)
                sp.wait_ge(fin_free, 16 * (NSEQ + 1))

            bodies(sp, prologue, body, tail)

        @block.tensor
        def _(pe):
            mm, tr = nc.tensor.matmul, nc.tensor.transpose

            def turn(s):
                pe.wait_ge(g_vec, s * KG + 20)
                for t in range(T):
                    tr(misc_b[0][:, t * P:(t + 1) * P], xn[:, t, :], ident[:, :])
                for t in range(T):
                    last = tr(misc_b[0][:, SEQ + t * P:SEQ + (t + 1) * P], z[:, t, :], ident[:, :])
                last.then_inc(g_tr, 1)

            def split(dst, s, t, w0, ready):
                hi, lo = hTh[:, t * P:(t + 1) * P], hTl[:, t * P:(t + 1) * P]
                mm(dst, hi, wh[:, w0:w0 + 512], start=True, stop=False)
                mm(dst, lo, wh[:, w0:w0 + 512], start=False, stop=False)
                mm(dst, hi, wl[:, w0:w0 + 512], start=False, stop=True).then_inc(ready, 1)

            def project(s, j):
                if j == 0:
                    pe.wait_ge(g_vec, (s + 1) * KG)
                if j >= 2:
                    pe.wait_ge(qk_raw, s * NJ + j - 1)
                t, w = divmod(j, 4)
                split(misc_b[j % 2][:, :], s, t, w * 512, qk_ready)

            def project_v(s, j):
                if j == 0:
                    pe.wait_ge(qk_raw, (s + 1) * NJ)
                    from_one(pe, o_vec, (s - 1) * KO)
                if j >= 2:
                    pe.wait_ge(v_lo, s * 2 * T + j - 1)
                t, w = divmod(j, 2)
                split(misc_b[j % 2][:, :], s, t, 2 * HD + w * 512, v_ready)

            def turn_qk(s, n):
                if n < 4:
                    pe.wait_ge(k_hi, s * 2 * T + n + 1)
                elif n < 8:
                    pe.wait_ge(q_lo, s * 2 * T + n - 3)
                else:
                    pe.wait_ge(k_lo, s * 2 * T + 2 * (n - 7))
                if n >= 2:
                    pe.wait_ge(t_done, s * NT + n - 1)
                dst = turn_b[n % 2][:, :].bitcast(F16)
                for m in range(8):
                    if n < 8:
                        t, h = (n % 4) // 2, (n % 2) * 8 + m
                    if 4 <= n < 8:
                        src = Qs[:, t, h // 2, 2 * (h % 2):2 * (h % 2) + 2, :].rearrange("p a d -> p (a d)")
                    elif n < 4:
                        src = Kh[:, t, h, :, :].rearrange("p a d -> p (a d)")
                    else:
                        src = Kl[:, n - 8, m * P:(m + 1) * P]
                    last = tr(dst[:, m * P:(m + 1) * P], src, ident16[:, :])
                last.then_inc(t_ready, 1)

            def scores(s, h, before):
                if h == 0:
                    pe.wait_ge(t_done, (s + 1) * NT)
                if h < 2 and before:
                    pe.wait_ge(gelu_done, (s - 1) * NE * FC - 2 * (1 - h))
                if h >= 2:
                    pe.wait_ge(ex_done, s * 2 * H + 2 * (h - 1))
                o, p0 = score_b[h % 2], DH * (h % 2)
                for t in range(T):
                    keys = (t + 1) * P
                    dst = o[:, t * P:t * P + keys]
                    q = QT[:, h, t * P:(t + 1) * P]
                    mm(dst, q, KT[:, h, 0:keys], start=True, stop=False)
                    mm(dst, q[p0:p0 + DH, :], KL[p0:p0 + DH, h // 2, 0:keys], start=False, stop=False)
                    last = mm(dst[:, t * P:keys], identb[:, :], maskb[:, :], start=False, stop=True)
                last.then_inc(sc_ready, 1)

            def turn_p(s, h):
                pe.wait_ge(p_lo, s * H + h + 1)
                dst = turn_b[h % 2][:, :].bitcast(F16)
                for n, src in enumerate((Ph, Pl)):
                    for m in range(3):
                        last = tr(dst[:, (3 * n + m) * P:(3 * n + m + 1) * P],
                                  src[:, h % 2, m * P:(m + 1) * P], ident16[:, :])
                last.then_inc(pt_ready, 1)

            def weigh(s, h, before):
                g = h // GH
                pe.wait_ge(*pt_copied(s, h))
                if h == 0:
                    pe.wait_ge(v_lo, (s + 1) * 2 * T)
                    if before:
                        pe.wait_ge(acc_done, (s - 1) * NE * T)
                if h == GH:
                    if not isinstance(s, int) or s > 0:
                        pe.wait_ge(o_vec, (s - 1) * KO + 11)
                if h % GH == 0 and g >= 2:
                    pe.wait_ge(ot_done, s * NG + g - 1)
                for t in range(T):
                    dst = sum_b[g % 2][:, (t * GH + h % GH) * DH:(t * GH + h % GH + 1) * DH]
                    terms = [(a, kb) for kb in range(t + 1) for a in ((0, Vh), (0, Vl), (1, Vh))]
                    for n, ((half, v), kb) in enumerate(terms):
                        last = mm(dst, PT[:, h % 2, half, t + kb, :], v[:, kb, h * DH:(h + 1) * DH],
                                  start=(n == 0), stop=(n == len(terms) - 1))
                last.then_inc(pv_done, 1)

            def turn_o(s, g):
                pe.wait_ge(on_done, s * NG + g + 1)
                for m in range(2):
                    for t in range(T):
                        last = tr(sum_b[g % 2][:, (m * T + t) * P:(m * T + t + 1) * P],
                                  On[:, g % 2, t, m * P:(m + 1) * P], ident[:, :])
                last.then_inc(ot_ready, 1)

            def output(s, part, before=True):
                o0, o1 = misc_b
                if part < T:
                    t = part
                    if t == 0:
                        pe.wait_ge(ot_done, (s + 1) * NG)
                        if before:
                            pe.wait_ge(acc_done, s * NE * T)
                    for m in range(HD // P):
                        last = mm(sum_b[1][:, t * P:(t + 1) * P], OT[:, m, t * P:(t + 1) * P],
                                  wos[:, m, :], start=(m == 0), stop=(m == HD // P - 1))
                    if t == T - 1:
                        last.then_inc(wo_ready, 1)
                elif part == 2:
                    pe.wait_ge(o_vec, s * KO + 10)
                    pe.wait_ge(xy_done, s + 1)
                    for t in range(T):
                        last = tr(sum_b[1][:, t * P:(t + 1) * P], z2[:, t, :], ident[:, :])
                    last.then_inc(o_tr, 1)
                elif part == 3:
                    pe.wait_ge(o_vec, s * KO + 11)
                    for t in range(T):
                        last = mm(o0[:, t * NE:(t + 1) * NE], h2T[:, t * P:(t + 1) * P], gws[:, :],
                                  start=True, stop=True)
                    last.then_inc(o_gate, 1)
                elif part == 4:
                    pe.wait_ge(o_vec, s * KO + 20)
                    for t in range(T):
                        last = tr(o1[:, t * P:(t + 1) * P], gate[:, t, :], ident[:, :])
                    last.then_inc(o_gT, 1)
                else:
                    pe.wait_ge(o_vec, s * KO + 21)
                    for t in range(T):
                        last = mm(o0[:, t * P:(t + 1) * P], gateT[0:NE, t * P:(t + 1) * P], b2s[:, :],
                                  start=True, stop=True)
                    last.then_inc(o_b2, 1)

            def expert_up(s, e):
                if e == 0:
                    pe.wait_ge(o_vec, s * KO + 13)
                for q in (2 * e, 2 * e + 1):
                    if q >= 2:
                        pe.wait_ge(gelu_done, s * NE * FC + 2 * (q - 1))
                    for m in range(2):
                        f = (2 * q + m) * P
                        dst = score_b[q % 2][:, m * SEQ:(m + 1) * SEQ]
                        mm(dst, w1h[:, f:f + P], h2h[:, :], start=True, stop=False)
                        mm(dst, w1h[:, f:f + P], h2l[:, :], start=False, stop=False)
                        last = mm(dst, w1l[:, f:f + P], h2h[:, :], start=False, stop=True)
                    last.then_inc(w1_ready, 1)

            def expert_down(s, e):
                pe.wait_ge(gelu_done, s * NE * FC + FC * (e + 1))
                if e >= 2:
                    pe.wait_ge(acc_done, s * NE * T + T * (e - 1))
                for t in range(T):
                    for m in range(FC):
                        last = mm(sum_b[e % 2][:, t * P:(t + 1) * P], hid[:, e % 2, m, t * P:(t + 1) * P],
                                  w2s[:, e * FC + m, :], start=(m == 0), stop=(m == FC - 1))
                    last.then_inc(w2_ready, 1)

            def step_sizes(s):
                pe.wait_ge(c_vec, s * KC + 3)
                pe.wait_ge(v_lo, (s + 1) * 2 * T)
                mm(misc_b[1][:, 0:SEQ], dtwT[:, :], xf[:, :], start=True, stop=True).then_inc(dt_ready, 1)

            def turn_y(s):
                pe.wait_ge(y_done, (s + 1) * DS)
                pe.wait_ge(wo_copied, s + 1)
                for t in range(T):
                    last = tr(sum_b[1][:, t * P:(t + 1) * P], y[:, t * P:(t + 1) * P], ident[:, :])
                last.then_inc(y_tr, 1)

            def heads(i, k, older):
                if k == 1:
                    scores(i, 2, older)
                if 3 <= k < H:
                    scores(i, k, older)
                if 5 <= k < H + 5:
                    weigh(i, k - 5, older)
                if 3 <= k < H + 3:
                    turn_p(i, k - 3)
                if k in (10, 14, 18):
                    turn_o(i, (k - 10) // GH)
                if k == 21:
                    turn_o(i, NG - 1)

            def prologue():
                pe.wait_ge(const_vec, 3)
                turn(0)
                pe.wait_ge(d_cols, 16 * 7)
                tr(misc_b[1][:, 0:D], dtw[:, :], ident[:, :])
                tr(misc_b[1][:, D:D + NE * FC], b1r[:, :], ident[0:NE * FC, 0:NE * FC]).then_inc(setup_tr, 1)
                pe.wait_ge(w_low, 1)
                pe.wait_ge(setup_vec, 1)
                for j in range(NJ):
                    project(0, j)
                for n in range(4):
                    turn_qk(0, n)
                pe.wait_ge(w_low, 2)
                for j in range(2 * T):
                    project_v(0, j)
                for n in range(4, NT):
                    turn_qk(0, n)
                pe.wait_ge(v_lo, 2 * T)
                turn(1)
                step_sizes(0)
                scores(0, 0, False)
                scores(0, 1, False)
                pe.wait_ge(d_w2, 16)
                pe.wait_ge(d_wo, 16)

            def body(i, older, old, new, newer):
                for k in range(H + 1):
                    heads(i, k, older)
                    if old and k in (1, 2):
                        output(i - 1, k - 1, older)
                    if old and k == 4:
                        turn_y(i - 1)
                    if old and k == 7:
                        output(i - 1, 2)
                    if new and 2 <= k < 2 + NJ:
                        if k == 3:
                            pe.wait_ge(tanh_done, i + 1)
                        project(i + 1, k - 2)
                    if old and k == 10:
                        if new:
                            pe.wait_ge(qk_raw, (i + 2) * NJ - 1)
                        output(i - 1, 3)
                    if old and k == 14:
                        if new:
                            pe.wait_ge(qk_raw, (i + 2) * NJ)
                        else:
                            pe.wait_ge(tanh_done, i + 1)
                        output(i - 1, 4)
                    if old and k == 15:
                        output(i - 1, 5)
                if new:
                    project_v(i + 1, 0)
                    project_v(i + 1, 1)
                if old:
                    pe.wait_ge(ex_done, (i + 1) * 2 * H)
                for m in range(NE + 2):
                    for k in (H + 1 + 2 * m, H + 2 + 2 * m):
                        heads(i, k, older)
                        if old and k % 2 == 1 and m < NE:
                            expert_up(i - 1, m)
                    if new and m in (NE - 1, NE):
                        scores(i + 1, m - NE + 1, old)
                    if not old and m == NE + 1:
                        pe.wait_ge(w1_low, 2)
                    if old and 1 <= m <= NE:
                        if m <= 2:
                            pe.wait_ge(ot_done, i * NG + 2 + m)
                        expert_down(i - 1, m - 1)
                    if new and m == 3:
                        project_v(i + 1, 2)
                        project_v(i + 1, 3)
                    if new and 2 <= m < 7:
                        turn_qk(i + 1, 2 * m - 4)
                        turn_qk(i + 1, 2 * m - 3)
                    if new and m == 6:
                        if newer:
                            pe.wait_ge(v_lo, (i + 2) * 2 * T)
                            turn(i + 2)
                        step_sizes(i + 1)

            def tail():
                output(LAST, 0)
                output(LAST, 1)
                turn_y(LAST)
                for part in range(2, 4):
                    output(LAST, part)
                for e in range(NE + 1):
                    if e < NE:
                        expert_up(LAST, e)
                    if e < 2:
                        output(LAST, 4 + e)
                    if e >= 1:
                        expert_down(LAST, e - 1)

            bodies(pe, prologue, body, tail)

        @block.scalar
        def _(act):
            fn = nc.scalar.activation

            def with_exp_and_ln():
                nc.scalar.preload_act_table_set("natural_log_exp_and_others")

            def with_gelu_and_tanh():
                nc.scalar.preload_act_table_set("gelu_apprx_tanh_and_others")

            def inverse_root(semaphore, at, src, ln, dst, eps):
                fn(ln, src, ACT.Ln, bias=eps).then_inc(semaphore, 1)
                act.wait_ge(semaphore, at + 1)
                fn(dst, ln, ACT.Exp, scale=-0.5).then_inc(semaphore, 1)

            def norm(s, n):
                act.wait_ge(g_vec, s * KG + (4, 14)[n])
                inverse_root(g_act, s * KGA + 2 * n, gmv[:, :, 1], gln[:, :], gy[:, :], eps_ln[:, :])

            def copy_raw(s, j):
                act.wait_ge(qk_ready, s * NJ + j + 1)
                fn(raw[:, j, :], misc_b[j % 2][:, :], ACT.Copy).then_inc(qk_raw, 1)

            def norm_qk(s):
                act.wait_ge(qk_sum, (s + 1) * NJ)
                inverse_root(n_act, s * 2, ssq[:, :], nln[:, :], ny[:, :], eps_l2[:, :])

            def v_high(s, j):
                t, w = divmod(j, 2)
                act.wait_ge(v_ready, s * 2 * T + j + 1)
                if j == 0:
                    from_one(act, pv_done, s * H)
                fn(Vh[:, t, w * 512:(w + 1) * 512], misc_b[j % 2][:, :], ACT.Copy,
                   scale=1.0 / WS).then_inc(v_hi, 1)

            def copy_turned(s, n):
                act.wait_ge(t_ready, s * NT + n + 1)
                dst, src = turned(n)
                fn(dst, src, ACT.Copy).then_inc(t_done, 1)

            def split_w1(half):
                act.wait_ge(d_w1, 16 * (half + 1))
                fn(w1h[:, half * W1COLS:(half + 1) * W1COLS], W132, ACT.Copy, scale=WS).then_inc(w1_high, 1)

            def root_o(s):
                act.wait_ge(o_vec, s * KO + 4)
                inverse_root(o_act, s * KOA, omv[:, :, 1], oln[:, :], oy[:, :], eps_ln[:, :])

            def copy_output(s):
                act.wait_ge(wo_ready, s + 1)
                fn(z2[:, :, :].rearrange("p t d -> p (t d)"), sum_b[1][:, 0:SEQ], ACT.Copy).then_inc(wo_copied, 1)

            def gate_exps(s):
                act.wait_ge(o_vec, s * KO + 17)
                for t in range(T):
                    fn(ge[:, t, :], gl[:, t, :], ACT.Exp, accum_out=gs[:, t:t + 1]).then_inc(o_act, 1)

            def exps(s, h):
                act.wait_ge(mx_done, (s * H + h + 1) * T)
                if h < 3:
                    from_one(act, p_lo, s * H)
                else:
                    act.wait_ge(p_lo, s * H + h - 2)
                for t in range(T):
                    keys = (t + 1) * P
                    fn(P32[:, h % 3, t * P:t * P + keys], score_b[h % 2][:, t * P:t * P + keys], ACT.Exp,
                       bias=mx[:, h % 2, t:t + 1],
                       accum_out=rs[:, h // GH, t, h % GH:h % GH + 1]).then_inc(ex_done, 1)

            def copy_pt(s, h):
                act.wait_ge(pt_ready, s * H + h + 1)
                from_one(act, pv_done, s * H + h - 1)
                fn(PT[:, h % 2, :, :, :].rearrange("p a b q -> p (a b q)"),
                   turn_b[h % 2][:, :].bitcast(F16)[:, 0:6 * P], ACT.Copy).then_inc(pt_act, 1)

            def copy_ot(s, g):
                act.wait_ge(ot_ready, s * NG + g + 1)
                if g == 0:
                    from_one(act, wo_ready, s)
                fn(OT[:, 2 * g:2 * g + 2, :].rearrange("p m q -> p (m q)"), sum_b[g % 2][:, :],
                   ACT.Copy).then_inc(ot_done, 1)

            def decay(s, d):
                if d == 0:
                    act.wait_ge(c_vec, s * KC + 5)
                fn(aexp[:, d, :], dt[:, :], ACT.Exp, scale=negA[:, d:d + 1]).then_inc(a_done, 1)

            def step_tanh(s):
                act.wait_ge(dt_ready, s + 1)
                fn(th[:, :], misc_b[1][:, 0:SEQ], ACT.Tanh, bias=half_dtb[:, :], scale=0.5
                   ).then_inc(tanh_done, 1)

            def gelus(s, e):
                for q in (2 * e, 2 * e + 1):
                    act.wait_ge(w1_ready, s * NE * 2 + q + 1)
                    if q % 2 == 0 and e >= 2:
                        act.wait_ge(w2_ready, s * NE * T + T * (e - 1))
                    for m in range(2):
                        f = 2 * q + m
                        fn(hid[:, e % 2, f % FC, :], score_b[q % 2][:, m * SEQ:(m + 1) * SEQ],
                           ACT.Gelu_apprx_tanh, bias=b1c[:, f:f + 1], scale=1.0 / WS).then_inc(gelu_done, 1)

            def last_norm(s):
                act.wait_ge(e_vec, s * KE + 4)
                inverse_root(e_act, s * 2, emv[:, :, 1], eln[:, :], ey[:, :], eps_ln[:, :])

            def prologue():
                for n, src in enumerate((ln_g, ln_b, dt_b, conv_b)):
                    act.dma_start(cols[:, n:n + 1], src.unsqueeze(1)).then_inc(d_cols, 16)
                act.dma_start(cols[:, 4:7], conv_w.rearrange("p a k -> p (a k)")).then_inc(d_cols, 16)
                act.dma_start(dtw[:, :], dt_w).then_inc(d_cols, 16)
                act.dma_start(b1r[:, :], b1.rearrange("e (c p) -> (e c) p", p=P)).then_inc(d_cols, 16)
                with_exp_and_ln()
                act.wait_ge(const_vec, 3)
                norm(0, 0)
                act.wait_ge(d_w, 48)
                fn(wh[:, 0:2 * HD], W32[:, 0:2 * HD], ACT.Copy, scale=WS).then_inc(w_high, 1)
                norm(0, 1)
                fn(wh[:, 2 * HD:3 * HD], W32[:, 2 * HD:3 * HD], ACT.Copy, scale=WS).then_inc(w_high, 1)
                act.wait_ge(d_small, 16 * 10)
                fn(spt[:, 0, :], al[:, :], ACT.Abs).then_inc(setup_act, 1)
                act.wait_ge(setup_act, 1)
                fn(spt[:, 1, :], spt[:, 0, :], ACT.Exp, scale=-1.0).then_inc(setup_act, 1)
                act.wait_ge(setup_act, 2)
                fn(spt[:, 2, :], spt[:, 1, :], ACT.Ln, bias=1.0).then_inc(setup_act, 1)
                act.wait_ge(w_low, 2)
                for j in range(NJ):
                    copy_raw(0, j)
                norm_qk(0)
                for n in range(4):
                    copy_turned(0, n)
                for j in range(2 * T):
                    v_high(0, j)
                for n in range(4, NT):
                    copy_turned(0, n)
                norm(1, 0)
                norm(1, 1)
                act.wait_ge(setup_vec, 4)
                with_gelu_and_tanh()
                step_tanh(0)
                with_exp_and_ln()

            def heads(i, k):
                if k - 4 in PT_ACT:
                    copy_pt(i, k - 4)
                if k in (11, 15, 19):
                    copy_ot(i, (k - 11) // GH)
                if k == 21:
                    copy_ot(i, NG - 1)

            def body(i, older, old, new, newer):
                for k in range(H + 1):
                    if k >= 1:
                        exps(i, k - 1)
                        decay(i, k - 1)
                    if new and 3 <= k < 3 + NJ:
                        copy_raw(i + 1, k - 3)
                    heads(i, k)
                    if old and k == 3:
                        copy_output(i - 1)
                    if older and k == 2:
                        last_norm(i - 2)
                    if newer and k == 3:
                        norm(i + 2, 0)
                    if old and k == 4:
                        root_o(i - 1)
                    if newer and k == 10:
                        norm(i + 2, 1)
                    if old and k == 12:
                        gate_exps(i - 1)
                    if new and k == 12:
                        norm_qk(i + 1)
                with_gelu_and_tanh()
                for m in range(NE + 2):
                    if not old and m in (2, 6):
                        split_w1(m // 4)
                    if new and m in (2, 4):
                        v_high(i + 1, m - 2)
                        v_high(i + 1, m - 1)
                    if new and 3 <= m < 8:
                        copy_turned(i + 1, 2 * m - 6)
                        copy_turned(i + 1, 2 * m - 5)
                    for k in (H + 1 + 2 * m, H + 2 + 2 * m):
                        heads(i, k)
                    if old and m < NE:
                        gelus(i - 1, m)
                    if new and m == 7:
                        step_tanh(i + 1)
                with_exp_and_ln()

            def tail():
                last_norm(LAST - 1)
                copy_output(LAST)
                root_o(LAST)
                gate_exps(LAST)
                with_gelu_and_tanh()
                for e in range(NE):
                    gelus(LAST, e)
                with_exp_and_ln()
                last_norm(LAST)

            bodies(act, prologue, body, tail)

        @block.gpsimd
        def _(pool):
            def square(s, j):
                square_on(pool, nc.gpsimd, s, j)

            def q_scaled(s, n):
                t, w = divmod(n, 2)
                pool.wait_ge(qk_sq, s * NJ + 4 * t + w + 1)
                nc.gpsimd.tensor_tensor(raw[:, 4 * t + w, :], raw[:, 4 * t + w, :],
                                        crow[:, w * 512:(w + 1) * 512], ALU.mult).then_inc(qc_done, 1)

            def q_low(s, n):
                t, w = divmod(n, 2)
                pool.wait_ge(q_hi, s * 2 * T + n + 1)
                pair = Qs[:, t, 4 * w:4 * w + 4, :, :]
                src = raw[:, 4 * t + w, :].rearrange("p (a h d) -> p a h d", h=2, d=DH)
                nc.gpsimd.tensor_tensor(pair[:, :, 1:3, :], src, pair[:, :, 0:4:3, :], ALU.subtract
                                        ).then_inc(q_lo, 1)

            def q_unit(s, n):
                pool.wait_ge(qc_done, s * 2 * T + n + 1)
                over_norm_on(pool, nc.gpsimd, s, n, 0, q_norm)

            def k_unit(s, n):
                over_norm_on(pool, nc.gpsimd, s, n, 1, k_norm)

            def k_low(s, n):
                k_low_on(pool, nc.gpsimd, s, n)

            def p_low(s, h):
                pool.wait_ge(p_hi, s * H + h + 1)
                nc.gpsimd.tensor_tensor(Pl[:, h % 2, :], P32[:, h % 3, :], Ph[:, h % 2, :], ALU.subtract
                                        ).then_inc(p_lo, 1)

            def x_bias(s):
                pool.wait_ge(xres_loaded, 16 * (s + 1))
                from_one(pool, xy_done, s)
                nc.gpsimd.tensor_tensor(xb[:, :, :], xres[:, :, :],
                                        brow[:, :].unsqueeze(1).broadcast_to([P, T, D]), ALU.add
                                        ).then_inc(xb_done, 1)

            def prologue():
                nc.gpsimd.memset(ident[:, :], 0.0).then_inc(const_pool, 1)
                nc.gpsimd.memset(mask[:, :], 0.0).then_inc(const_pool, 1)
                pool.wait_ge(const_pool, 2)
                nc.gpsimd.affine_select(out=ident[:, :], in_=ident[:, :], compare_op=ALU.not_equal, fill=1.0,
                                        base=0, pattern=[[-1, P]], channel_multiplier=1
                                        ).then_inc(const_pool, 1)
                nc.gpsimd.affine_select(out=mask[:, :], in_=mask[:, :], compare_op=ALU.is_ge, fill=MASKED,
                                        base=0, pattern=[[-1, P]], channel_multiplier=1
                                        ).then_inc(const_pool, 1)
                pool.wait_ge(d_small, 16 * 10)
                pool.wait_ge(setup_vec, 2)
                for n in range(2 * T):
                    q_scaled(0, n)
                for n in range(2 * T):
                    q_unit(0, n)
                for n in range(2 * T):
                    q_low(0, n)

            def body(i, older, old, new, newer):
                for k in range(H + 2):
                    if old and k == 0:
                        x_bias(i - 1)
                    if new and 4 <= k < 4 + NJ:
                        square(i + 1, k - 4)
                    if 2 <= k:
                        p_low(i, k - 2)
                if new:
                    for n in range(2 * T):
                        k_unit(i + 1, n)
                    for n in range(2 * T):
                        q_scaled(i + 1, n)
                        q_unit(i + 1, n)
                        if n % 2 == 1:
                            q_low(i + 1, n - 1)
                            q_low(i + 1, n)
                    for n in range(2 * T):
                        k_low(i + 1, n)

            def tail():
                x_bias(LAST)

            bodies(pool, prologue, body, tail)

        @block.vector
        def _(dve):
            V = nc.vector

            def root_step(n, semaphore, done, root_ready, ve, y0, a, b_, dst, src, eps):
                if n == 0:
                    dve.wait_ge(semaphore, done)
                    V.tensor_scalar(ve, src, eps, None, ALU.add).then_inc(semaphore, 1)
                    dve.wait_ge(*root_ready)
                    dve.wait_ge(semaphore, done + 1)
                    V.scalar_tensor_tensor(a, y0, -0.5, ve, ALU.mult, ALU.mult).then_inc(semaphore, 1)
                elif n == 1:
                    dve.wait_ge(semaphore, done + 2)
                    V.tensor_tensor(b_, a, y0, ALU.mult).then_inc(semaphore, 1)
                else:
                    dve.wait_ge(semaphore, done + 3)
                    V.scalar_tensor_tensor(dst, b_, 1.5, y0, ALU.add, ALU.mult).then_inc(semaphore, 1)

            def stats(semaphore, src, st6):
                for t in range(T):
                    V.bn_stats(st6[:, t, :], src(t)).then_inc(semaphore, 1)

            def aggregate(semaphore, done, st6, mv):
                dve.wait_ge(semaphore, done)
                V.memset(pad[:, :], 0.0)
                for t in range(T):
                    V.bn_aggr(mv[:, t, :], st6[:, t, :]).then_inc(semaphore, 1)

            def normalise(semaphore, done, dst, src, mv, r):
                dve.wait_ge(semaphore, done)
                for t in range(T):
                    V.tensor_scalar(dst[:, t, :], src(t), mv[:, t, 0:1], r[:, t:t + 1],
                                    ALU.subtract, ALU.mult).then_inc(semaphore, 1)

            def g_step(s, n):
                at = s * KG
                if n < 12:
                    src = (lambda t: xin[:, t, :]) if n < 6 else (lambda t: xn[:, t, :])
                    at += 10 * (n // 6)
                if n in (0, 6):
                    if n == 0:
                        dve.wait_ge(x_loaded, 16 * (s + 1))
                    else:
                        dve.wait_ge(g_vec, at)
                    stats(g_vec, src, gst)
                elif n in (1, 7):
                    aggregate(g_vec, at + 2, gst, gmv)
                elif n in (2, 3, 4, 8, 9, 10):
                    root_step(n % 6 - 2, g_vec, at + 4, (g_act, s * KGA + 2 + 2 * (n // 6)), gve[:, :],
                              gy[:, :], gu[:, :], gw[:, :], gr[:, :], gmv[:, :, 1], LN_EPS)
                elif n in (5, 11):
                    normalise(g_vec, at + 8, (xn, z)[n // 6], src, gmv, gr)
                elif n == 12:
                    dve.wait_ge(g_tr, s + 1)
                    V.tensor_copy(xnT[:, 1:SEQ + 1], misc_b[0][:, 0:SEQ]).then_inc(g_vec, 1)
                    V.tensor_scalar(hT[:, :], misc_b[0][:, SEQ:2 * SEQ], lng, lnb, ALU.mult, ALU.add
                                    ).then_inc(g_vec, 1)
                elif n == 13:
                    dve.wait_ge(g_vec, at + 22)
                    V.tensor_copy(hTh[:, :], hT[:, :]).then_inc(g_vec, 1)
                else:
                    dve.wait_ge(g_vec, at + 23)
                    V.tensor_tensor(hTl[:, :], hT[:, :], hTh[:, :], ALU.subtract).then_inc(g_vec, 1)

            def qk_sums(s, j):
                dve.wait_ge(qk_sq, s * NJ + j + 1)
                V.tensor_reduce(ssq[:, j * 8:(j + 1) * 8], sq[:, j % 2, :].rearrange("p (h d) -> p h d", d=DH),
                                AX.X, ALU.add).then_inc(qk_sum, 1)

            def q_high(s, n):
                t, w = divmod(n, 2)
                dve.wait_ge(q_norm, s * 2 * T + n + 1)
                V.tensor_copy(Qs[:, t, 4 * w:4 * w + 4, 0:4:3, :],
                              raw[:, 4 * t + w, :].rearrange("p (a h d) -> p a h d", h=2, d=DH)).then_inc(q_hi, 1)

            def norm_step(s, n):
                if n == 0:
                    dve.wait_ge(qk_sum, (s + 1) * NJ)
                from_zero = s * KN
                if n == 0:
                    V.tensor_scalar(nve[:, :], ssq[:, :], L2_EPS * WS * WS, None, ALU.add).then_inc(n_vec, 1)
                    dve.wait_ge(n_act, s * 2 + 2)
                    dve.wait_ge(n_vec, from_zero + 1)
                    V.scalar_tensor_tensor(nu[:, :], ny[:, :], -0.5, nve[:, :], ALU.mult, ALU.mult
                                           ).then_inc(n_vec, 1)
                elif n == 1:
                    dve.wait_ge(n_vec, from_zero + 2)
                    V.tensor_tensor(nw[:, :], nu[:, :], ny[:, :], ALU.mult).then_inc(n_vec, 1)
                else:
                    dve.wait_ge(n_vec, from_zero + 3)
                    V.scalar_tensor_tensor(nr[:, :], nw[:, :], 1.5, ny[:, :], ALU.add, ALU.mult
                                           ).then_inc(n_vec, 1)

            def k_high(s, n):
                t, w = divmod(n, 2)
                dve.wait_ge(k_norm, s * 2 * T + n + 1)
                V.tensor_copy(Kh[:, t, w * 8:(w + 1) * 8, :, :],
                              raw[:, 4 * t + 2 + w, :].rearrange("p (h d) -> p h d", d=DH).unsqueeze(2)
                              .broadcast_to([P, 8, 2, DH])).then_inc(k_hi, 1)

            def v_low(s, j):
                t, w = divmod(j, 2)
                dve.wait_ge(v_hi, s * 2 * T + j + 1)
                V.scalar_tensor_tensor(Vl[:, t, w * 512:(w + 1) * 512], misc_b[j % 2][:, :], 1.0 / WS,
                                       Vh[:, t, w * 512:(w + 1) * 512], ALU.mult, ALU.subtract
                                       ).then_inc(v_lo, 1)

            def maxima(s, h):
                dve.wait_ge(sc_ready, s * H + h + 1)
                for t in range(T):
                    V.tensor_reduce(mx[:, h % 2, t:t + 1], score_b[h % 2][:, t * P:t * P + (t + 1) * P], AX.X,
                                    ALU.max, negate=True).then_inc(mx_done, 1)

            def p_high(s, h):
                dve.wait_ge(ex_done, s * 2 * H + 2 * h + 2)
                from_one(dve, pt_ready, s * H + h - 1)
                V.tensor_copy(Ph[:, h % 2, :], P32[:, h % 3, :]).then_inc(p_hi, 1)

            def copy_pt(s, h):
                dve.wait_ge(pt_ready, s * H + h + 1)
                from_one(dve, pv_done, s * H + h - 1)
                V.tensor_copy(PT[:, h % 2, :, :, :].rearrange("p a b q -> p (a b q)"),
                              turn_b[h % 2][:, :].bitcast(F16)[:, 0:6 * P]).then_inc(pt_dve, 1)

            def inverse_sums(s, g):
                dve.wait_ge(ex_done, s * 2 * H + 2 * GH * (g + 1))
                V.reciprocal(rr[:, g % 2, :], rs[:, g, :, :].rearrange("p t h -> p (t h)")).then_inc(rr_done, 1)

            def divide(s, g):
                dve.wait_ge(rr_done, s * NG + g + 1)
                dve.wait_ge(pv_done, s * H + GH * (g + 1))
                V.tensor_tensor(On[:, g % 2, :, :].rearrange("p t (h d) -> p (t h) d", d=DH),
                                sum_b[g % 2][:, :].rearrange("p (a d) -> p a d", d=DH),
                                rr[:, g % 2, :].unsqueeze(2).broadcast_to([P, T * GH, DH]), ALU.mult
                                ).then_inc(on_done, 1)

            def o_step(s, n):
                at = s * KO
                o0, o1 = misc_b
                src = lambda t: z2[:, t, :]
                if n == 0:
                    dve.wait_ge(wo_copied, s + 1)
                    stats(o_vec, src, ost)
                elif n == 1:
                    aggregate(o_vec, at + 2, ost, omv)
                elif n <= 4:
                    root_step(n - 2, o_vec, at + 4, (o_act, s * KOA + 2), ove[:, :], oy[:, :], ou[:, :],
                              ow[:, :], orr[:, :], omv[:, :, 1], LN_EPS)
                elif n == 5:
                    normalise(o_vec, at + 8, z2, src, omv, orr)
                elif n == 6:
                    dve.wait_ge(o_tr, s + 1)
                    V.tensor_scalar(h2T[:, :], sum_b[1][:, 0:SEQ], lng, lnb, ALU.mult, ALU.add
                                    ).then_inc(o_vec, 1)
                elif n == 7:
                    dve.wait_ge(o_vec, at + 11)
                    V.tensor_copy(h2h[:, :], h2T[:, :]).then_inc(o_vec, 1)
                elif n == 8:
                    dve.wait_ge(o_vec, at + 12)
                    V.tensor_tensor(h2l[:, :], h2T[:, :], h2h[:, :], ALU.subtract).then_inc(o_vec, 1)
                elif n == 9:
                    dve.wait_ge(o_gate, s + 1)
                    V.tensor_tensor(gl[:, :, :], o0[:, 0:T * NE].rearrange("p (t e) -> p t e", t=T),
                                    gbrow[:, :].unsqueeze(1).broadcast_to([P, T, NE]), ALU.add
                                    ).then_inc(o_vec, 1)
                elif n == 10:
                    dve.wait_ge(o_vec, at + 14)
                    V.tensor_reduce(gm[:, :], gl[:, :, :], AX.X, ALU.max).then_inc(o_vec, 1)
                elif n == 11:
                    dve.wait_ge(o_vec, at + 15)
                    for t in range(T):
                        V.tensor_scalar(gl[:, t, :], gl[:, t, :], gm[:, t:t + 1], None, ALU.subtract
                                        ).then_inc(o_vec, 1)
                elif n == 12:
                    dve.wait_ge(o_act, (s + 1) * KOA)
                    V.reciprocal(grs[:, :], gs[:, :]).then_inc(o_vec, 1)
                elif n == 13:
                    dve.wait_ge(o_vec, at + 18)
                    for t in range(T):
                        V.tensor_scalar(gate[:, t, 0:NE], ge[:, t, :], grs[:, t:t + 1], None, ALU.mult
                                        ).then_inc(o_vec, 1)
                elif n == 14:
                    dve.wait_ge(o_gT, s + 1)
                    V.tensor_copy(gateT[:, :], o1[:, 0:SEQ]).then_inc(o_vec, 1)
                else:
                    dve.wait_ge(o_b2, s + 1)
                    V.tensor_copy(acc[:, :, :].rearrange("p t d -> p (t d)"), o0[:, 0:SEQ]
                                  ).then_inc(o_vec, 1)

            def add_expert(s, e, t):
                if t == 0:
                    dve.wait_ge(w2_ready, s * NE * T + (e + 1) * T)
                if e > 0:
                    dve.wait_ge(acc_done, s * NE * T + (e - 1) * T + t + 1)
                elif t == 0:
                    dve.wait_ge(o_vec, (s + 1) * KO)
                V.scalar_tensor_tensor(acc[:, t, :], sum_b[e % 2][:, t * P:(t + 1) * P],
                                       gate[:, t, e:e + 1], acc[:, t, :], ALU.mult, ALU.add
                                       ).then_inc(acc_done, 1)

            def convolve(s, n):
                if n == 0:
                    V.tensor_scalar(cv[:, 0, :], xnT[:, 1:SEQ + 1], cols[:, 5:6], cb, ALU.mult, ALU.add
                                    ).then_inc(c_vec, 1)
                else:
                    dve.wait_ge(c_vec, s * KC + n)
                    V.scalar_tensor_tensor((cv[:, 1, :], xf[:, :])[n - 1], xnT[:, 2 * n - 2:2 * n - 2 + SEQ],
                                           cols[:, 2 * n + 2:2 * n + 3], cv[:, n - 1, :], ALU.mult, ALU.add
                                           ).then_inc(c_vec, 1)

            def step_inputs(s, n):
                if n == 0:
                    dve.wait_ge(tanh_done, s + 1)
                    half = 0.5 * (DT_MAX - DT_MIN)
                    V.tensor_scalar(dt[:, :], th[:, :], half, half + DT_MIN, ALU.mult, ALU.add
                                    ).then_inc(c_vec, 1)
                else:
                    dve.wait_ge(c_vec, s * KC + 4)
                    V.tensor_tensor(u[:, :], dt[:, :], xf[:, :], ALU.mult).then_inc(c_vec, 1)

            def scan(s, d):
                dve.wait_ge(a_done, s * DS + d + 1)
                if d == 0:
                    dve.wait_ge(c_vec, (s + 1) * KC)
                from_one(dve, y_done, s * DS + d - 1)
                V.tensor_tensor_scan(st[:, d % 2, :], aexp[:, d, :], u[:, :], 0.0, ALU.mult, ALU.add
                                     ).then_inc(scan_done, 1)

            def add_state(s, d):
                dve.wait_ge(scan_done, s * DS + d + 1)
                if d == 0:
                    V.tensor_scalar(y[:, :], st[:, 0, :], bc[:, 0:1], None, ALU.mult).then_inc(y_done, 1)
                else:
                    dve.wait_ge(y_done, s * DS + d)
                    V.scalar_tensor_tensor(y[:, :], st[:, d % 2, :], bc[:, d:d + 1], y[:, :],
                                           ALU.mult, ALU.add).then_inc(y_done, 1)

            def e_step(s, n):
                at = s * KE
                if n == 0:
                    dve.wait_ge(acc_done, (s + 1) * NE * T)
                    stats(e_vec, lambda t: acc[:, t, :], est)
                elif n == 1:
                    aggregate(e_vec, at + 2, est, emv)
                elif n <= 4:
                    root_step(n - 2, e_vec, at + 4, (e_act, s * 2 + 2), eve[:, :], ey[:, :], eu[:, :],
                              ew[:, :], er[:, :], emv[:, :, 1], LN_EPS)
                elif n == 5:
                    normalise(e_vec, at + 8, e1, lambda t: acc[:, t, :], emv, er)
                elif n == 6:
                    dve.wait_ge(e_vec, at + 10)
                    V.tensor_tensor(e2[:, :, :], e1[:, :, :],
                                    grow[:, :].unsqueeze(1).broadcast_to([P, T, D]), ALU.mult
                                    ).then_inc(e_vec, 1)
                else:
                    dve.wait_ge(e_vec, at + 11)
                    dve.wait_ge(fin_free, 16 * (s + 1))
                    dve.wait_ge(xy_done, s + 1)
                    V.tensor_tensor(fin[:, :, :], e2[:, :, :], xy[:, :, :], ALU.add).then_inc(e_vec, 1)

            def add_y(s):
                dve.wait_ge(xb_done, s + 1)
                dve.wait_ge(y_tr, s + 1)
                from_one(dve, e_vec, s * KE)
                V.tensor_tensor(xy[:, :, :].rearrange("p t d -> p (t d)"), sum_b[1][:, 0:SEQ],
                                xb[:, :, :].rearrange("p t d -> p (t d)"), ALU.add).then_inc(xy_done, 1)

            def prologue():
                V.memset(pad[:, :], 0.0).then_inc(fin_free, 16)
                V.memset(eps_ln[:, :], LN_EPS)
                V.memset(eps_l2[:, :], L2_EPS * WS * WS)
                V.memset(xnT[:, :], 0.0)
                V.memset(gate[:, :, :].rearrange("p t e -> p (t e)"), 0.0)
                dve.wait_ge(const_pool, 4)
                V.tensor_copy(ident16[:, :], ident[:, :]).then_inc(const_vec, 1)
                V.tensor_copy(identb[:, :], ident[:, :]).then_inc(const_vec, 1)
                V.tensor_copy(maskb[:, :], mask[:, :]).then_inc(const_vec, 1)
                for n in range(12):
                    g_step(0, n)
                for n, (c0, c1) in enumerate(((0, 2 * HD), (2 * HD, 3 * HD))):
                    dve.wait_ge(w_high, n + 1)
                    V.scalar_tensor_tensor(wl[:, c0:c1], W32[:, c0:c1], WS, wh[:, c0:c1],
                                           ALU.mult, ALU.subtract).then_inc(w_low, 1)
                    if n == 0:
                        dve.wait_ge(d_cols, 16 * 7)
                        for part in range(12, 15):
                            g_step(0, part)
                        dve.wait_ge(setup_tr, 1)
                        V.tensor_copy(dtwT[:, :], misc_b[1][:, 0:D])
                        V.tensor_copy(b1c[:, :], misc_b[1][:, D:D + NE * FC]).then_inc(setup_vec, 1)
                V.tensor_scalar(half_dtb[:, :], dtb, 0.5, None, ALU.mult)
                dve.wait_ge(d_small, 16 * 10)
                V.tensor_tensor(bc[:, :], bs[:, :], cs[:, :], ALU.mult)
                V.scalar_tensor_tensor(crow[:, :], crow[:, :], QK_SCALE, krow, ALU.mult, ALU.mult
                                       ).then_inc(setup_vec, 1)
                dve.wait_ge(setup_vec, 2)
                for j in range(NJ):
                    square_on(dve, V, 0, j)
                    qk_sums(0, j)
                    if j < 3:
                        convolve(0, j)
                dve.wait_ge(setup_act, 3)
                V.scalar_tensor_tensor(spt[:, 3, :], al[:, :], 0.0, spt[:, 2, :], ALU.max, ALU.add
                                       ).then_inc(setup_vec, 1)
                dve.wait_ge(setup_vec, 3)
                V.tensor_scalar(negA[:, :], spt[:, 3, :], -1.0, None, ALU.mult).then_inc(setup_vec, 1)
                for n in range(3):
                    norm_step(0, n)
                for n in range(2 * T):
                    over_norm_on(dve, V, 0, n, 1, k_norm)
                    k_high(0, n)
                for n in range(2 * T):
                    q_high(0, n)
                for j in range(2 * T):
                    v_low(0, j)
                for n in range(2 * T):
                    k_low_on(dve, V, 0, n)
                for n in range(15):
                    g_step(1, n)
                maxima(0, 0)
                maxima(0, 1)
                step_inputs(0, 0)
                step_inputs(0, 1)

            def split_w1(half):
                dve.wait_ge(w1_high, half + 1)
                V.scalar_tensor_tensor(w1l[:, half * W1COLS:(half + 1) * W1COLS], W132, WS,
                                       w1h[:, half * W1COLS:(half + 1) * W1COLS], ALU.mult, ALU.subtract
                                       ).then_inc(w1_low, 1)

            E_AT = {(1, 0): 0, (1, 2): 1, (3, 1): 2, (3, 2): 3, (4, 0): 4, (4, 2): 5, (5, 0): 6, (5, 2): 7}
            G_AT = {(2, 0): 0, (2, 2): 1, (7, 1): 2, (7, 2): 3, (8, 1): 4, (9, 0): 5, (9, 1): 6, (9, 2): 7,
                    (12, 0): 8, (12, 1): 9, (12, 2): 10}
            O_AT = {(4, 1): 0, (4, 2): 1, (6, 0): 2, (6, 1): 3, (6, 2): 4, (7, 0): 5, (8, 0): 6, (8, 2): 7,
                    (10, 0): 8, (11, 0): 9, (11, 1): 10, (11, 2): 11, (13, 0): 12, (13, 2): 13, (15, 0): 14,
                    (16, 1): 15}
            N_AT = {(14, 0): 0, (14, 1): 1, (14, 2): 2}

            def body(i, older, old, new, newer):
                def between(k, place):
                    if older and (k, place) in E_AT:
                        e_step(i - 2, E_AT[k, place])
                    if newer and (k, place) in G_AT:
                        g_step(i + 2, G_AT[k, place])
                    if old and (k, place) in O_AT:
                        o_step(i - 1, O_AT[k, place])
                    if new and (k, place) in N_AT:
                        norm_step(i + 1, N_AT[k, place])

                for k in range(H + 1):
                    j = k - 5
                    if k >= 3:
                        maxima(i, k - 1)
                    if k >= 2:
                        p_high(i, k - 2)
                    if old and k == 6:
                        add_y(i - 1)
                    between(k, 0)
                    if k >= 9 and k % GH == 1:
                        inverse_sums(i, (k - 9) // GH)
                    if k >= 4 and k - 4 not in PT_ACT:
                        copy_pt(i, k - 4)
                    if new and 0 <= j < NJ:
                        qk_sums(i + 1, j)
                    between(k, 1)
                    if k >= 9 and k % GH == 1:
                        divide(i, (k - 9) // GH)
                    between(k, 2)
                for m in range(NE + 2):
                    if m == 0:
                        p_high(i, H - 1)
                        inverse_sums(i, 2)
                        divide(i, 2)
                        copy_pt(i, H - 3)
                        copy_pt(i, H - 2)
                        inverse_sums(i, 3)
                    if new and m == NE:
                        maxima(i + 1, 0)
                        step_inputs(i + 1, 0)
                        step_inputs(i + 1, 1)
                    if new and m == NE + 1:
                        maxima(i + 1, 1)
                    if old and m >= 2:
                        add_expert(i - 1, m - 2, 0)
                    if m == 1:
                        copy_pt(i, H - 1)
                    if new and m in (1, 2):
                        k_high(i + 1, 2 * m - 2)
                        k_high(i + 1, 2 * m - 1)
                    if new and m in (2, 3):
                        q_high(i + 1, 2 * m - 4)
                        q_high(i + 1, 2 * m - 3)
                    if m < NE:
                        scan(i, 2 * m)
                    if old and m >= 2:
                        add_expert(i - 1, m - 2, 1)
                    if m < NE:
                        scan(i, 2 * m + 1)
                        add_state(i, 2 * m)
                    if newer and m == 0:
                        g_step(i + 2, 11)
                    if not old and m in (2, 6):
                        split_w1(m // 4)
                    if new and m in (2, 4):
                        v_low(i + 1, m - 2)
                        v_low(i + 1, m - 1)
                    if new and m in (2, 3, 4):
                        convolve(i + 1, m - 2)
                    if newer and m == 7:
                        g_step(i + 2, 12)
                    if m < NE:
                        add_state(i, 2 * m + 1)
                    if newer and m == 7:
                        g_step(i + 2, 13)
                        g_step(i + 2, 14)
                    if m == 1:
                        divide(i, 3)

            def tail():
                for n in range(8):
                    e_step(LAST - 1, n)
                add_y(LAST)
                for n in range(16):
                    o_step(LAST, n)
                for e in range(NE):
                    add_expert(LAST, e, 0)
                    add_expert(LAST, e, 1)
                for n in range(8):
                    e_step(LAST, n)

            bodies(dve, prologue, body, tail)


_INS = ['x', 'a_log', 'b', 'c', 'dt_w', 'dt_b', 'conv_w', 'conv_b']
_FFN = ['ln_g', 'ln_b', 'Wq', 'Wk', 'Wv', 'q_scale', 'k_scale', 'Wo', 'gate_w', 'gate_b', 'w1', 'b1', 'w2', 'b2']


def kernel(**inputs):
    import concourse.bacc as bacc
    from concourse.bass_utils import run_bass_kernel_spmd

    nc = bacc.Bacc("TRN2", target_bir_lowering=False, num_devices=1)
    arrays, args = {}, []
    for name in [f"L0_attn_{n}" for n in _INS] + [f"L0_ffn_{n}" for n in _FFN]:
        a = np.ascontiguousarray(inputs[name])
        arrays[f"in_{name}"] = a
        args.append(nc.dram_tensor(f"in_{name}", a.shape, mybir.dt.from_np(a.dtype), kind="ExternalInput").ap())
    shape = inputs["L0_attn_x"].shape
    args.append(nc.dram_tensor("out_dram", shape, F32, kind="ExternalOutput").ap())
    build(nc, *args)
    r = run_bass_kernel_spmd(nc, [arrays], core_ids=[0])
    return r.results[0]["out_dram"]
```
